# Optimizing a Trainium2 kernel written in Bass

```python
import numpy as np
import jax
import jax.numpy as jnp

def _softmax(x, axis=-1):
    return jax.nn.softmax(x, axis=axis)

def _gelu(x):
    return jax.nn.gelu(x, approximate=True)

def _silu(x):
    return jax.nn.silu(x)

def _sigmoid(x):
    return jax.nn.sigmoid(x)

def _layernorm(x, axis=-1, eps=1e-05):
    m = jnp.mean(x, axis=axis, keepdims=True)
    v = jnp.var(x, axis=axis, keepdims=True)
    return (x - m) / jnp.sqrt(v + eps)

def _scatter_add(tgt, idx, src, axis=0):
    return tgt.at[idx].add(src)

def _segment_sum(src, seg, n):
    return jax.ops.segment_sum(src, seg, n)
kernel_name = 'mk_seq_postln_d1_jaxref_r4_5dc73c'

def setup_inputs(seed: int=0):
    np.random.seed(seed)
    _w = jnp.asarray

    def _L0_attn_setup():
        import jax, jax.numpy as jnp
        import numpy as np
        B, L, D = (8, 1024, 256)
        key = jax.random.key(seed)
        k1, k2, k3, k4, k5 = jax.random.split(key, 5)
        s = 1.0 / np.sqrt(D)
        return {'x': jax.random.normal(k1, (B, L, D), dtype=jnp.float32), 'Wg': jax.random.uniform(k2, (1, D), dtype=jnp.float32, minval=-s, maxval=s), 'bg': jax.random.uniform(k3, (1,), dtype=jnp.float32, minval=-s, maxval=s), 'Wout': jax.random.uniform(k4, (D, D), dtype=jnp.float32, minval=-s, maxval=s), 'bout': jax.random.uniform(k5, (D,), dtype=jnp.float32, minval=-s, maxval=s)}
    _L0_attn_in = _L0_attn_setup()

    def _L0_ffn_setup():
        import jax, jax.numpy as jnp
        import numpy as np
        DIM = 256

        def _reference_tuple_inner(x, W_r, W_k, W_v, mu_r, mu_k):
            B, T, C = x.shape
            x_prev = jnp.concatenate([jnp.zeros((B, 1, C), x.dtype), x[:, :-1, :]], axis=1)
            xr = mu_r * x + (1.0 - mu_r) * x_prev
            xk = mu_k * x + (1.0 - mu_k) * x_prev
            r = jax.nn.sigmoid(jnp.einsum('btc,dc->btd', xr, W_r))
            k = jnp.einsum('btc,dc->btd', xk, W_k)
            k_act = jnp.square(jax.nn.relu(k))
            out = r * jnp.einsum('btc,dc->btd', k_act, W_v)
            new_state = x[:, -1, :]
            return (out, new_state)
        key = jax.random.key(seed)
        ks = jax.random.split(key, 6)
        B, T, C = (8, 512, DIM)
        x = jax.random.normal(ks[0], (B, T, C), dtype=jnp.float32)
        s = 1.0 / np.sqrt(C)
        W_r = jax.random.uniform(ks[1], (C, C), jnp.float32, -s, s)
        W_k = jax.random.uniform(ks[2], (C, C), jnp.float32, -s, s)
        W_v = jax.random.uniform(ks[3], (C, C), jnp.float32, -s, s)
        mu_r = jax.random.uniform(ks[4], (C,), jnp.float32)
        mu_k = jax.random.uniform(ks[5], (C,), jnp.float32)
        return {'x': x, 'W_r': W_r, 'W_k': W_k, 'W_v': W_v, 'mu_r': mu_r, 'mu_k': mu_k}
    _L0_ffn_in = _L0_ffn_setup()
    _d = {'L0_attn_x': _L0_attn_in['x'], 'L0_attn_Wg': _L0_attn_in['Wg'], 'L0_attn_bg': _L0_attn_in['bg'], 'L0_attn_Wout': _L0_attn_in['Wout'], 'L0_attn_bout': _L0_attn_in['bout'], 'L0_ffn_W_r': _L0_ffn_in['W_r'], 'L0_ffn_W_k': _L0_ffn_in['W_k'], 'L0_ffn_W_v': _L0_ffn_in['W_v'], 'L0_ffn_mu_r': _L0_ffn_in['mu_r'], 'L0_ffn_mu_k': _L0_ffn_in['mu_k']}
    _x0 = _d['L0_attn_x']
    _d['L0_attn_x'] = jax.random.normal(jax.random.fold_in(jax.random.key(seed), 1), (2, 2048, 256), dtype=_x0.dtype)
    del _x0
    return _d

def reference(L0_attn_x, L0_attn_Wg, L0_attn_bg, L0_attn_Wout, L0_attn_bout, L0_ffn_W_r, L0_ffn_W_k, L0_ffn_W_v, L0_ffn_mu_r, L0_ffn_mu_k):

    def _L0_attn_ref(x, Wg, bg, Wout, bout):
        import jax, jax.numpy as jnp
        import numpy as np
        B, L, D = (8, 1024, 256)
        g = jax.nn.sigmoid(jnp.einsum('bld,d->bl', x, Wg[0]) + bg[0])
        g_t = jnp.transpose(g)[:, :, None]
        x_t = jnp.transpose(x, (1, 0, 2))
        h0 = jnp.zeros((x.shape[0], x.shape[2]), dtype=x.dtype)

        def step(h, inp):
            gt, xt = inp
            h = (1.0 - gt) * h + gt * xt
            return (h, h)
        _, hs = jax.lax.scan(step, h0, (g_t, x_t))
        H = jnp.transpose(hs, (1, 0, 2))
        out = jnp.einsum('bld,ed->ble', H, Wout) + bout
        return out

    def _L0_ffn_ref(x, W_r, W_k, W_v, mu_r, mu_k):
        import jax, jax.numpy as jnp
        import numpy as np
        DIM = 256

        def _reference_tuple_inner(x, W_r, W_k, W_v, mu_r, mu_k):
            B, T, C = x.shape
            x_prev = jnp.concatenate([jnp.zeros((B, 1, C), x.dtype), x[:, :-1, :]], axis=1)
            xr = mu_r * x + (1.0 - mu_r) * x_prev
            xk = mu_k * x + (1.0 - mu_k) * x_prev
            r = jax.nn.sigmoid(jnp.einsum('btc,dc->btd', xr, W_r))
            k = jnp.einsum('btc,dc->btd', xk, W_k)
            k_act = jnp.square(jax.nn.relu(k))
            out = r * jnp.einsum('btc,dc->btd', k_act, W_v)
            new_state = x[:, -1, :]
            return (out, new_state)
        return _reference_tuple_inner(x, W_r, W_k, W_v, mu_r, mu_k)[0]
    x = L0_attn_x
    x = _layernorm(x + _L0_attn_ref(x, L0_attn_Wg, L0_attn_bg, L0_attn_Wout, L0_attn_bout), axis=-1)
    x = _layernorm(x + _L0_ffn_ref(x, L0_ffn_W_r, L0_ffn_W_k, L0_ffn_W_v, L0_ffn_mu_r, L0_ffn_mu_k), axis=-1)
    return x

_drawn_inputs = setup_inputs


def setup_inputs(seed=0):
    import zlib

    import numpy as np

    out = dict(_drawn_inputs(seed))
    spreads = {}
    factors = {'L0_ffn_W_r': 3.084, 'L0_ffn_mu_r': 6.452}
    for name, (base, spread) in spreads.items():
        noise = np.random.default_rng([zlib.crc32(name.encode()), seed]).standard_normal(out[name].shape)
        drawn = base * np.exp(spread * noise) if base else spread * noise
        out[name] = jnp.asarray(drawn.astype(out[name].dtype))
    for name, factor in factors.items():
        out[name] = (out[name] * factor).astype(out[name].dtype)
    return out
```

```python
from contextlib import ExitStack

import concourse.bass as bass
from concourse import mybir

P = 128
GROUP = 512
TILES = GROUP // P
ALU = mybir.AluOpType
ACT = mybir.ActivationFunctionType
F32 = mybir.dt.float32
EPS = 1e-5


class Step:

    def __init__(self, j, b):
        self.j, self.b = j, b

    def after(self, n=1):
        return Step(self.j + (self.b + n) // 2, (self.b + n) % 2)

    def count(self, each=1, part=None):
        return (self.j * 2 + self.b) * each + (each if part is None else part)


def build(nc, x, Wg, bg, WoutT, bout, WrT, WkT, WvT, mus, out):
    B, T, C = x.shape
    HALVES = C // P
    STEPS = B * T // GROUP
    assert B == 2 and C == 2 * P and T % GROUP == 0 and STEPS >= 6

    x_steps = x.rearrange("b (j k p) c -> b j p k c", p=P, k=TILES)
    out_steps = out.rearrange("b (j k p) c -> b j p k c", p=P, k=TILES)

    def rows(w):
        return w.rearrange("(h p) n -> p h n", p=P)

    with ExitStack() as ctx:
        def sb(name, shape):
            return ctx.enter_context(nc.sbuf_tensor(name, shape, F32))

        def psum(name, shape):
            return ctx.enter_context(nc.psum_tensor(name, shape, F32))

        def sem(name):
            return ctx.enter_context(nc.semaphore(name))

        wout = sb("wout", [P, HALVES, C])
        wk = sb("wk", [P, HALVES, C])
        wr = sb("wr", [P, HALVES, C])
        wv = sb("wv", [P, HALVES, C])
        wg_rows = sb("wg_rows", [P, C])
        bout_rows = sb("bout_rows", [P, 2, C])
        bg_col = sb("bg_col", [P, 1])
        mu = sb("mu", [P, 2, HALVES])
        one_minus_mu = sb("one_minus_mu", [P, 2, HALVES])
        ident = sb("ident", [P, P])
        minus_half = sb("minus_half", [P, TILES])
        minus_one = sb("minus_one", [P, TILES])
        eps = sb("eps", [P, TILES])
        settled_pool = sb("settled_pool", [P, 1])
        settled_dve = sb("settled_dve", [P, 1])

        x_tok = [sb(f"x_tok{b}", [P, TILES, C]) for b in range(2)]
        x_bias = [sb(f"x_bias{b}", [P, TILES, C]) for b in range(2)]
        gated_x = [sb(f"gated_x{b}", [P, TILES, C]) for b in range(2)]
        gate = [sb(f"gate{b}", [P, 3, TILES]) for b in range(2)]
        decay = [sb(f"decay{b}", [P, GROUP]) for b in range(2)]
        hidden = [sb(f"hidden{b}", [P, HALVES, GROUP]) for b in range(2)]
        y_tok = [sb(f"y_tok{b}", [P, TILES, C]) for b in range(2)]
        shifted = [sb(f"shifted{b}", [P, 2, HALVES, GROUP + 1]) for b in range(2)]
        out_tok = [sb(f"out_tok{b}", [P, TILES, C]) for b in range(2)]
        dot_terms = sb("dot_terms", [P, 2, TILES, C])
        z1 = sb("z1", [P, TILES, C])
        z2 = sb("z2", [P, TILES, C])
        stats = sb("stats", [P, 2, TILES, 6])
        moments = sb("moments", [P, 2, TILES, 2])
        norm = sb("norm", [P, 2, 4, TILES])
        mixed = sb("mixed", [P, 2, HALVES, GROUP])
        relu_k = sb("relu_k", [P, HALVES, GROUP])
        k_act = sb("k_act", [P, HALVES, GROUP])
        r_gate = sb("r_gate", [P, TILES, C])
        rv = sb("rv", [P, TILES, C])

        pair_yT_r = [psum(f"pair_yT_r{h}", [P, GROUP]) for h in range(2)]
        pair_gx_attn = [psum(f"pair_gx_attn{h}", [P, GROUP]) for h in range(2)]
        pair_k_v = [psum(f"pair_k_v{h}", [P, GROUP]) for h in range(2)]
        decay_ps = [psum(f"decay_ps{b}", [P, GROUP]) for b in range(2)]

        s_x = [sem(f"s_x{b}") for b in range(2)]
        s_gate_w = sem("s_gate_w")
        s_bout = sem("s_bout")
        s_wout = sem("s_wout")
        s_mu = sem("s_mu")
        s_wk = sem("s_wk")
        s_wr = sem("s_wr")
        s_wv = sem("s_wv")
        s_ident = sem("s_ident")
        s_const = sem("s_const")
        s_zeros = sem("s_zeros")
        s_omm = sem("s_omm")
        s_dot = sem("s_dot")
        s_gate = sem("s_gate")
        s_one_minus = sem("s_one_minus")
        s_gx = sem("s_gx")
        s_xb = sem("s_xb")
        s_decay_t = sem("s_decay_t")
        s_gx_t = sem("s_gx_t")
        s_decay = sem("s_decay")
        s_scan = sem("s_scan")
        s_attn = sem("s_attn")
        s_z1 = sem("s_z1")
        s_st1 = sem("s_st1")
        s_mom1 = sem("s_mom1")
        s_ln1 = sem("s_ln1")
        s_y = sem("s_y")
        s_yT = sem("s_yT")
        s_carry = sem("s_carry")
        s_shift = sem("s_shift")
        s_mix_k = sem("s_mix_k")
        s_mix_r = sem("s_mix_r")
        s_k = sem("s_k")
        s_relu = sem("s_relu")
        s_kact = sem("s_kact")
        s_r = sem("s_r")
        s_sig = sem("s_sig")
        s_v = sem("s_v")
        s_rv = sem("s_rv")
        s_z2 = sem("s_z2")
        s_st2 = sem("s_st2")
        s_mom2 = sem("s_mom2")
        s_ln2 = sem("s_ln2")
        s_out = sem("s_out")
        s_stored = [sem(f"s_stored{b}") for b in range(2)]

        def pair(t, h):
            return t[:, 2 * h:2 * h + 2, :].rearrange("p k c -> p (k c)")

        block = ctx.enter_context(nc.Block())

        @block.sync
        def _(sp):
            def load(step):
                if not (isinstance(step.j, int) and step.j == 0):
                    before = step.after(-2)
                    sp.wait_ge(s_dot, before.count())
                    sp.wait_ge(s_gx, before.count())
                    sp.wait_ge(s_xb, before.count())
                sp.dma_start(x_tok[step.b][:, :, :], x_steps[step.b, step.j]).then_inc(s_x[step.b], 16)

            def store(step):
                sp.wait_ge(s_out, step.count())
                sp.dma_start(out_steps[step.b, step.j], out_tok[step.b][:, :, :]).then_inc(s_stored[step.b], 16)

            load(Step(0, 0))
            load(Step(0, 1))
            sp.dma_start(wout[:, :, :], rows(WoutT)).then_inc(s_wout, 16)
            sp.dma_start(wk[:, :, :], rows(WkT)).then_inc(s_wk, 16)
            load(Step(1, 0))
            with sp.Fori(0, STEPS // 2 - 2) as i:
                for b in range(2):
                    load(Step(i, b).after(3))
                    store(Step(i, b))
            load(Step(STEPS // 2 - 1, 1))
            for j in (STEPS // 2 - 2, STEPS // 2 - 1):
                for b in range(2):
                    store(Step(j, b))
            for b in range(2):
                sp.wait_ge(s_stored[b], 16 * (STEPS // 2))

        @block.gpsimd
        def _(pool):
            gp = nc.gpsimd
            gp.memset(ident[:, :], 0.0).then_inc(s_const, 1)
            pool.wait_ge(s_const, 1)
            gp.affine_select(out=ident[:, :], in_=ident[:, :], compare_op=ALU.not_equal, fill=1.0, base=0,
                             pattern=[[-1, P]], channel_multiplier=1).then_inc(s_ident, 1)
            for tile, value in ((minus_half, -0.5), (minus_one, -1.0), (eps, EPS)):
                gp.memset(tile[:, :], value).then_inc(s_const, 1)
            pool.wait_ge(s_const, 4)

            def residual_bias(step):
                b = step.b
                pool.wait_ge(s_x[b], (step.j + 1) * 16)
                if not (isinstance(step.j, int) and step.j == 0):
                    pool.wait_ge(s_z1, step.after(-2).count(2))
                for h in range(2):
                    last = gp.tensor_tensor(pair(x_bias[b], h), pair(x_tok[b], h),
                                            bout_rows[:, :, :].rearrange("p k c -> p (k c)"), ALU.add)
                last.then_inc(s_xb, 1)

            def scale_and_offset(n, s_small, s_moments, step):
                pool.wait_ge(s_moments, step.count())
                gp.tensor_tensor(norm[:, n, 0, :], moments[:, n, :, 1], eps[:, :], ALU.add).then_inc(s_small, 1)
                gp.tensor_tensor(norm[:, n, 1, :], moments[:, n, :, 0], minus_one[:, :], ALU.mult).then_inc(s_small, 1)
                pool.wait_ge(s_small, step.count(4, 2))
                gp.tensor_tensor(norm[:, n, 2, :], norm[:, n, 0, :], minus_half[:, :], ALU.pow).then_inc(s_small, 1)
                pool.wait_ge(s_small, step.count(4, 3))
                gp.tensor_tensor(norm[:, n, 3, :], norm[:, n, 1, :], norm[:, n, 2, :], ALU.mult).then_inc(s_small, 1)
                pool.wait_ge(s_small, step.count(4, 4))
                gp.tensor_tensor(settled_pool[:, :], norm[:, n, 3, 0:1], norm[:, n, 2, 0:1], ALU.mult)

            def norm1(step):
                scale_and_offset(0, s_ln1, s_mom1, step)
                for k in range(TILES):
                    gp.tensor_scalar(y_tok[step.b][:, k, :], z1[:, k, :], norm[:, 0, 2, k:k + 1],
                                     norm[:, 0, 3, k:k + 1], ALU.mult, ALU.add).then_inc(s_y, 1)

            def residual2(step):
                pool.wait_ge(s_out, step.after(-1).count())
                for h in range(2):
                    pool.wait_ge(s_rv, step.count(2, h + 1))
                    gp.tensor_tensor(pair(z2, h), pair(rv, h), pair(y_tok[step.b], h), ALU.add).then_inc(s_z2, 1)

            def norm2(step):
                if not (isinstance(step.j, int) and step.j == 0):
                    pool.wait_ge(s_stored[step.b], step.j * 16)
                scale_and_offset(1, s_ln2, s_mom2, step)
                for k in range(TILES):
                    last = gp.tensor_scalar(out_tok[step.b][:, k, :], z2[:, k, :], norm[:, 1, 2, k:k + 1],
                                            norm[:, 1, 3, k:k + 1], ALU.mult, ALU.add)
                last.then_inc(s_out, 1)

            def body(step, to_come):
                if to_come >= 2:
                    residual_bias(step.after(2))
                if to_come >= 1:
                    norm1(step.after(1))
                residual2(step)
                norm2(step)

            pool.wait_ge(s_bout, 32)
            residual_bias(Step(0, 0))
            residual_bias(Step(0, 1))
            norm1(Step(0, 0))
            with pool.Fori(0, STEPS // 2 - 1) as i:
                for b in range(2):
                    body(Step(i, b), 2)
            for b in range(2):
                body(Step(STEPS // 2 - 1, b), 1 - b)

        @block.scalar
        def _(act):
            sc = nc.scalar
            act.dma_start(wg_rows[:, :], Wg.to_broadcast([P, C])).then_inc(s_gate_w, 16)
            act.dma_start(bg_col[:, :], bg.rearrange("(a n) -> a n", a=1).to_broadcast([P, 1])).then_inc(s_gate_w, 16)
            for h in range(2):
                act.dma_start(bout_rows[:, h, :], bout.rearrange("(a n) -> a n", a=1).to_broadcast([P, C])).then_inc(s_bout, 16)
            act.dma_start(mu[:, :, :], mus).then_inc(s_mu, 16)
            act.dma_start(wr[:, :, :], rows(WrT)).then_inc(s_wr, 16)
            act.dma_start(wv[:, :, :], rows(WvT)).then_inc(s_wv, 16)

            def gate_and_gated_x(step):
                b = step.b
                act.wait_ge(s_dot, step.count())
                if not (isinstance(step.j, int) and step.j == 0):
                    act.wait_ge(s_decay_t, step.after(-2).count())
                    act.wait_ge(s_gx_t, step.after(-2).count(2))
                sc.activation(gate[b][:, 1, :], gate[b][:, 0, :], ACT.Sigmoid, bias=bg_col[:, 0:1]).then_inc(s_gate, 1)
                act.wait_ge(s_gate, step.count())
                sc.activation(gate[b][:, 2, :], gate[b][:, 1, :], ACT.Identity, scale=-1.0, bias=1.0).then_inc(s_one_minus, 1)
                for k in range(TILES):
                    last = sc.activation(gated_x[b][:, k, :], x_tok[b][:, k, :], ACT.Copy, scale=gate[b][:, 1, k:k + 1])
                last.then_inc(s_gx, 1)

            def copy_decay(step):
                b = step.b
                act.wait_ge(s_decay_t, step.count())
                if not (isinstance(step.j, int) and step.j == 0):
                    act.wait_ge(s_scan, step.after(-2).count(2))
                sc.activation(decay[b][:, :], decay_ps[b][:, :], ACT.Copy).then_inc(s_decay, 1)

            def shift(step):
                b = step.b
                w = shifted[b]
                if not (isinstance(step.j, int) and step.j == 0):
                    act.wait_ge(s_mix_r, step.after(-2).count(2))
                sc.activation(w[:, :, :, 0:1], w[:, :, :, GROUP:GROUP + 1], ACT.Copy).then_inc(s_carry, 1)
                act.wait_ge(s_carry, step.count())
                for h in range(HALVES):
                    act.wait_ge(s_yT, step.count(2, h + 1))
                    for n in range(2):
                        last = sc.activation(w[:, n, h, 1:GROUP + 1], pair_yT_r[h][:, :], ACT.Copy,
                                             scale=one_minus_mu[:, n, h:h + 1])
                    last.then_inc(s_shift, 1)

            def relu_squared(step):
                for h in range(HALVES):
                    act.wait_ge(s_k, step.count(2, h + 1))
                    sc.activation(relu_k[:, h, :], pair_k_v[h][:, :], ACT.Relu).then_inc(s_relu, 1)
                for h in range(HALVES):
                    act.wait_ge(s_relu, step.count(2, h + 1))
                    sc.activation(k_act[:, h, :], relu_k[:, h, :], ACT.Square).then_inc(s_kact, 1)

            def r_sigmoid(step):
                for h in range(2):
                    act.wait_ge(s_r, step.count(2, h + 1))
                    sc.activation(pair(r_gate, h), pair_yT_r[h][:, :], ACT.Sigmoid).then_inc(s_sig, 1)

            def body(step, to_come):
                if to_come >= 2:
                    gate_and_gated_x(step.after(2))
                relu_squared(step)
                r_sigmoid(step)
                if to_come >= 2:
                    copy_decay(step.after(2))
                if to_come >= 1:
                    shift(step.after(1))

            act.wait_ge(s_gate_w, 32)
            gate_and_gated_x(Step(0, 0))
            copy_decay(Step(0, 0))
            gate_and_gated_x(Step(0, 1))
            copy_decay(Step(0, 1))
            act.wait_ge(s_omm, 1)
            act.wait_ge(s_zeros, 4)
            shift(Step(0, 0))
            with act.Fori(0, STEPS // 2 - 1) as i:
                for b in range(2):
                    body(Step(i, b), 2)
            for b in range(2):
                body(Step(STEPS // 2 - 1, b), 1 - b)

        @block.vector
        def _(dve):
            v = nc.vector

            def gate_dot(step):
                b = step.b
                dve.wait_ge(s_x[b], (step.j + 1) * 16)
                if not (isinstance(step.j, int) and step.j == 0):
                    dve.wait_ge(s_gate, step.after(-2).count())
                for k in range(TILES):
                    last = v.tensor_tensor_reduce(out=dot_terms[:, b, k, :], in0=x_tok[b][:, k, :], in1=wg_rows[:, :],
                                                  scale=1.0, scalar=0.0, op0=ALU.mult, op1=ALU.add,
                                                  accum_out=gate[b][:, 0, k:k + 1])
                last.then_inc(s_dot, 1)

            def scan(step):
                b = step.b
                dve.wait_ge(s_decay, step.count())
                if not (isinstance(step.j, int) and step.j == 0):
                    dve.wait_ge(s_scan, step.after(-2).count(2))
                    dve.wait_ge(s_attn, step.after(-2).count(2))
                for h in range(HALVES):
                    dve.wait_ge(s_gx_t, step.count(2, h + 1))
                    v.tensor_tensor_scan(hidden[b][:, h, :], decay[b][:, :], pair_gx_attn[h][:, :],
                                         hidden[b][:, h, GROUP - 1:GROUP], ALU.mult, ALU.add).then_inc(s_scan, 1)

            def tile_stats(n, z, s_ready, s_st, s_mom, step):
                for k in range(TILES):
                    if k % 2 == 0:
                        dve.wait_ge(s_ready, step.count(2, k // 2 + 1))
                    last = v.bn_stats(stats[:, n, k, :], z[:, k, :])
                last.then_inc(s_st, 1)
                dve.wait_ge(s_st, step.count())
                v.tensor_copy(settled_dve[:, :], stats[:, n, 0, 0:1])
                for k in range(TILES):
                    last = v.bn_aggr(moments[:, n, k, :], stats[:, n, k, :])
                last.then_inc(s_mom, 1)

            def residual1(step):
                dve.wait_ge(s_xb, step.count())
                for h in range(2):
                    dve.wait_ge(s_attn, step.count(2, h + 1))
                    v.tensor_tensor(pair(z1, h), pair_gx_attn[h][:, :], pair(x_bias[step.b], h), ALU.add).then_inc(s_z1, 1)
                tile_stats(0, z1, s_z1, s_st1, s_mom1, step)

            def mix(step):
                for n, s_mix in ((0, s_mix_k), (1, s_mix_r)):
                    for h in range(HALVES):
                        dve.wait_ge(s_shift, step.count(2, h + 1))
                        v.scalar_tensor_tensor(out=mixed[:, n, h, :], in0=pair_yT_r[h][:, :], scalar=mu[:, n, h:h + 1],
                                               in1=shifted[step.b][:, n, h, 0:GROUP], op0=ALU.mult,
                                               op1=ALU.add).then_inc(s_mix, 1)

            def gate_v(step):
                for h in range(2):
                    dve.wait_ge(s_v, step.count(2, h + 1))
                    dve.wait_ge(s_sig, step.count(2, h + 1))
                    v.tensor_tensor(pair(rv, h), pair_k_v[h][:, :], pair(r_gate, h), ALU.mult).then_inc(s_rv, 1)

            def body(step, to_come):
                if to_come >= 2:
                    gate_dot(step.after(2))
                if to_come >= 1:
                    residual1(step.after(1))
                if to_come >= 2:
                    scan(step.after(2))
                gate_v(step)
                if to_come >= 1:
                    mix(step.after(1))
                tile_stats(1, z2, s_z2, s_st2, s_mom2, step)

            for b in range(2):
                v.memset(hidden[b][:, :, GROUP - 1:GROUP], 0.0).then_inc(s_zeros, 1)
                v.memset(shifted[b][:, :, :, GROUP:GROUP + 1], 0.0).then_inc(s_zeros, 1)
            dve.wait_ge(s_gate_w, 32)
            gate_dot(Step(0, 0))
            gate_dot(Step(0, 1))
            dve.wait_ge(s_mu, 16)
            v.tensor_scalar(one_minus_mu[:, :, :], mu[:, :, :], -1.0, 1.0, ALU.mult, ALU.add).then_inc(s_omm, 1)
            dve.wait_ge(s_omm, 1)
            dve.wait_ge(s_zeros, 4)
            scan(Step(0, 0))
            residual1(Step(0, 0))
            scan(Step(0, 1))
            mix(Step(0, 0))
            with dve.Fori(0, STEPS // 2 - 1) as i:
                for b in range(2):
                    body(Step(i, b), 2)
            for b in range(2):
                body(Step(STEPS // 2 - 1, b), 1 - b)

        @block.tensor
        def _(pe):
            t = nc.tensor

            def transpose_gated(step):
                b = step.b
                pe.wait_ge(s_one_minus, step.count())
                if not (isinstance(step.j, int) and step.j == 0):
                    pe.wait_ge(s_decay, step.after(-2).count())
                for k in range(TILES):
                    last = t.transpose(decay_ps[b][:, k * P:(k + 1) * P],
                                       gate[b][:, 2, k:k + 1].to_broadcast([P, P]), ident[:, :])
                last.then_inc(s_decay_t, 1)
                pe.wait_ge(s_gx, step.count())
                if not (isinstance(step.j, int) and step.j == 0 and b == 0):
                    pe.wait_ge(s_z1, step.after(-1).count(2))
                for h in range(HALVES):
                    for k in range(TILES):
                        last = t.transpose(pair_gx_attn[h][:, k * P:(k + 1) * P],
                                           gated_x[b][:, k, h * P:(h + 1) * P], ident[:, :])
                    last.then_inc(s_gx_t, 1)

            def token_product(banks, lhs, w, s_done):
                for h in range(2):
                    for k in (2 * h, 2 * h + 1):
                        for c in range(HALVES):
                            last = t.matmul(banks[h][:, (k % 2) * C:(k % 2 + 1) * C], lhs[:, c, k * P:(k + 1) * P],
                                            w[:, c, :], start=(c == 0), stop=(c == HALVES - 1))
                    last.then_inc(s_done, 1)

            def attn(step):
                pe.wait_ge(s_scan, step.count(2))
                token_product(pair_gx_attn, hidden[step.b], wout, s_attn)

            def transpose_y(step):
                pe.wait_ge(s_y, step.count(4))
                if not (isinstance(step.j, int) and step.j == 0 and step.b == 0):
                    pe.wait_ge(s_sig, step.after(-1).count(2))
                for h in range(HALVES):
                    for k in range(TILES):
                        last = t.transpose(pair_yT_r[h][:, k * P:(k + 1) * P],
                                           y_tok[step.b][:, k, h * P:(h + 1) * P], ident[:, :])
                    last.then_inc(s_yT, 1)

            def k_product(step):
                pe.wait_ge(s_mix_k, step.count(2))
                if not (isinstance(step.j, int) and step.j == 0 and step.b == 0):
                    pe.wait_ge(s_rv, step.after(-1).count(2))
                for h in range(HALVES):
                    for c in range(HALVES):
                        last = t.matmul(pair_k_v[h][:, :], wk[:, c, h * P:(h + 1) * P], mixed[:, 0, c, :],
                                        start=(c == 0), stop=(c == HALVES - 1))
                    last.then_inc(s_k, 1)

            def r_product(step):
                pe.wait_ge(s_mix_r, step.count(2))
                token_product(pair_yT_r, mixed[:, 1], wr, s_r)

            def v_product(step):
                pe.wait_ge(s_kact, step.count(2))
                token_product(pair_k_v, k_act, wv, s_v)

            def body(step, to_come):
                transpose_y(step)
                if to_come >= 1:
                    attn(step.after(1))
                k_product(step)
                r_product(step)
                if to_come >= 2:
                    transpose_gated(step.after(2))
                v_product(step)

            pe.wait_ge(s_ident, 1)
            transpose_gated(Step(0, 0))
            pe.wait_ge(s_wout, 16)
            attn(Step(0, 0))
            transpose_gated(Step(0, 1))
            pe.wait_ge(s_wk, 16)
            pe.wait_ge(s_wr, 16)
            pe.wait_ge(s_wv, 16)
            with pe.Fori(0, STEPS // 2 - 1) as i:
                for b in range(2):
                    body(Step(i, b), 2)
            for b in range(2):
                body(Step(STEPS // 2 - 1, b), 1 - b)


def kernel(L0_attn_x, L0_attn_Wg, L0_attn_bg, L0_attn_Wout, L0_attn_bout, L0_ffn_W_r, L0_ffn_W_k, L0_ffn_W_v,
           L0_ffn_mu_r, L0_ffn_mu_k):
    import numpy as np
    import concourse.bacc as bacc
    from concourse.bass_utils import run_bass_kernel_spmd

    nc = bacc.Bacc("TRN2", target_bir_lowering=False, num_devices=1)
    arrays = {
        "x": L0_attn_x, "Wg": L0_attn_Wg, "bg": L0_attn_bg, "WoutT": np.transpose(L0_attn_Wout), "bout": L0_attn_bout,
        "WrT": np.transpose(L0_ffn_W_r), "WkT": np.transpose(L0_ffn_W_k), "WvT": np.transpose(L0_ffn_W_v),
        "mus": np.transpose(np.stack([L0_ffn_mu_k, L0_ffn_mu_r]).reshape(2, -1, P), (2, 0, 1)),
    }
    arrays = {n: np.ascontiguousarray(a) for n, a in arrays.items()}
    ins = [nc.dram_tensor(n, a.shape, mybir.dt.from_np(a.dtype), kind="ExternalInput").ap() for n, a in arrays.items()]
    out = nc.dram_tensor("out", arrays["x"].shape, F32, kind="ExternalOutput").ap()
    build(nc, *ins, out)
    ran = run_bass_kernel_spmd(nc, [arrays], core_ids=[0])
    return ran.results[0]["out"]
```

```python
from contextlib import ExitStack

import concourse.bass as bass
from concourse import mybir

P = 128
GROUP = 512
TILES = GROUP // P
ALU = mybir.AluOpType
ACT = mybir.ActivationFunctionType
F32 = mybir.dt.float32
F32R = mybir.dt.float32r
EPS = 1e-5
LO_ROW = 32
WARM_UP = (12, 4, 14)


class Step:

    def __init__(self, j, b):
        self.j, self.b = j, b

    def after(self, n=1):
        return Step(self.j + (self.b + n) // 2, (self.b + n) % 2)

    def count(self, each=1, part=None):
        return (self.j * 2 + self.b) * each + (each if part is None else part)


def build(nc, x, Wg, bg, WoutT, bout, WrT, WkT, WvT, mus, out):
    B, T, C = x.shape
    HALVES = C // P
    STEPS = B * T // GROUP
    assert B == 2 and C == 2 * P and T % GROUP == 0 and STEPS >= 6

    x_steps = x.rearrange("b (j k p) c -> b j p k c", p=P, k=TILES)
    out_steps = out.rearrange("b (j k p) c -> b j p k c", p=P, k=TILES)

    def rows(w):
        return w.rearrange("(h p) n -> p h n", p=P)

    with ExitStack() as ctx:
        def sb(name, shape, dtype=F32):
            return ctx.enter_context(nc.sbuf_tensor(name, shape, dtype))

        def psum(name, shape):
            return ctx.enter_context(nc.psum_tensor(name, shape, F32))

        def sem(name):
            return ctx.enter_context(nc.semaphore(name))

        wout = sb("wout", [P, HALVES, C])
        wk = sb("wk", [P, HALVES, C])
        wr = sb("wr", [P, HALVES, C])
        wv = sb("wv", [P, HALVES, C])
        wg_rows = sb("wg_rows", [P, C])
        wout_hi = sb("wout_hi", [P, HALVES, C], F32R)
        wout_lo = sb("wout_lo", [P, HALVES, C], F32R)
        wk_hi = sb("wk_hi", [P, HALVES, C], F32R)
        wk_lo = sb("wk_lo", [P, HALVES, C], F32R)
        wv_hi = sb("wv_hi", [P, HALVES, C], F32R)
        wv_lo = sb("wv_lo", [P, HALVES, C], F32R)
        bout_row = sb("bout_row", [P, C])
        bout_parts = sb("bout_parts", [P, C], F32R)
        bout_hi = sb("bout_hi", [P, C], F32R)
        ones = sb("ones", [P, P], F32R)
        bg_col = sb("bg_col", [P, 1])
        mu = sb("mu", [P, 2, HALVES])
        one_minus_mu = sb("one_minus_mu", [P, 2, HALVES])
        ident = sb("ident", [P, P])
        minus_half = sb("minus_half", [P, TILES])
        minus_one = sb("minus_one", [P, TILES])
        eps = sb("eps", [P, TILES])
        settled_pool = sb("settled_pool", [P, 1])
        settled_dve = sb("settled_dve", [P, 1])

        x_tok = [sb(f"x_tok{b}", [P, TILES, C]) for b in range(2)]
        gated_x = [sb(f"gated_x{b}", [P, TILES, C]) for b in range(2)]
        gate = [sb(f"gate{b}", [P, 3, TILES]) for b in range(2)]
        decay = [sb(f"decay{b}", [P, GROUP]) for b in range(2)]
        hidden = [sb(f"hidden{b}", [P, HALVES, GROUP]) for b in range(2)]
        y_tok = [sb(f"y_tok{b}", [P, TILES, C]) for b in range(2)]
        shifted = [sb(f"shifted{b}", [P, 2, HALVES, GROUP + 1]) for b in range(2)]
        z2 = [sb(f"z2_{b}", [P, TILES, C]) for b in range(2)]
        out_last = sb("out_last", [P, TILES, C])
        out_tok = [sb(f"out_tok{b}", [P, TILES, C]) for b in range(2)]
        dot_terms = sb("dot_terms", [P, 2, TILES, C])
        z1 = sb("z1", [P, TILES, C])
        stats = sb("stats", [P, 2, TILES, 6])
        moments = sb("moments", [P, 2, TILES, 2])
        norm = sb("norm", [P, 2, 4, TILES])
        mixed = sb("mixed", [P, 2, HALVES, GROUP])
        mixed_hi = sb("mixed_hi", [P, HALVES, GROUP], F32R)
        mixed_lo = sb("mixed_lo", [P, HALVES, GROUP], F32R)
        hidden_hi = [sb(f"hidden_hi{b}", [P, HALVES, GROUP], F32R) for b in range(2)]
        hidden_lo = [sb(f"hidden_lo{b}", [P, HALVES, GROUP], F32R) for b in range(2)]
        relu_k = sb("relu_k", [P, HALVES, GROUP])
        k_act = sb("k_act", [P, HALVES, GROUP])
        k_hi = sb("k_hi", [P, HALVES, GROUP], F32R)
        k_lo = sb("k_lo", [P, HALVES, GROUP], F32R)
        r_gate = sb("r_gate", [P, TILES, C])
        rv = sb("rv", [P, TILES, C])

        pair_yT_r = [psum(f"pair_yT_r{h}", [P, GROUP]) for h in range(2)]
        pair_gx_attn = [psum(f"pair_gx_attn{h}", [P, GROUP]) for h in range(2)]
        pair_k_v = [psum(f"pair_k_v{h}", [P, GROUP]) for h in range(2)]
        decay_ps = [psum(f"decay_ps{b}", [P, GROUP]) for b in range(2)]

        s_x = [sem(f"s_x{b}") for b in range(2)]
        s_x_first = [sem(f"s_x_first{h}") for h in range(2)]
        s_gate_w = sem("s_gate_w")
        s_bout = sem("s_bout")
        s_wout = sem("s_wout")
        s_mu = sem("s_mu")
        s_wk = sem("s_wk")
        s_wr = sem("s_wr")
        s_wv = sem("s_wv")
        s_ident = sem("s_ident")
        s_const = sem("s_const")
        s_zeros = sem("s_zeros")
        s_omm = sem("s_omm")
        s_bias_zero = sem("s_bias_zero")
        s_bias_hi = sem("s_bias_hi")
        s_bias = sem("s_bias")
        s_wout_hi = sem("s_wout_hi")
        s_wout_lo = sem("s_wout_lo")
        s_wk_hi = sem("s_wk_hi")
        s_wk_lo = sem("s_wk_lo")
        s_wv_hi = sem("s_wv_hi")
        s_wv_lo = sem("s_wv_lo")
        s_dot = sem("s_dot")
        s_gate = sem("s_gate")
        s_one_minus = sem("s_one_minus")
        s_gx = sem("s_gx")
        s_decay_t = sem("s_decay_t")
        s_gx_t = sem("s_gx_t")
        s_decay = sem("s_decay")
        s_scan = sem("s_scan")
        s_hidden_hi = sem("s_hidden_hi")
        s_hidden_lo = sem("s_hidden_lo")
        s_attn = sem("s_attn")
        s_z1 = sem("s_z1")
        s_st1 = sem("s_st1")
        s_mom1 = sem("s_mom1")
        s_ln1 = sem("s_ln1")
        s_y = sem("s_y")
        s_yT = sem("s_yT")
        s_carry = sem("s_carry")
        s_shift = sem("s_shift")
        s_mix_k = sem("s_mix_k")
        s_mix_r = sem("s_mix_r")
        s_mixed_hi = sem("s_mixed_hi")
        s_mixed_lo = sem("s_mixed_lo")
        s_k = sem("s_k")
        s_relu = sem("s_relu")
        s_kact = sem("s_kact")
        s_k_hi = sem("s_k_hi")
        s_k_lo = sem("s_k_lo")
        s_r = sem("s_r")
        s_sig = sem("s_sig")
        s_v = sem("s_v")
        s_rv = sem("s_rv")
        s_z2 = sem("s_z2")
        s_st2 = sem("s_st2")
        s_mom2 = sem("s_mom2")
        s_ln2 = sem("s_ln2")
        s_out = sem("s_out")
        s_last_act = sem("s_last_act")
        s_last_dve = sem("s_last_dve")
        s_last_stored = [sem(f"s_last_stored{h}") for h in range(2)]
        s_stored = [sem(f"s_stored{b}") for b in range(2)]

        def starts(step, before):
            return isinstance(step.j, int) and 2 * step.j + step.b < before

        def all_steps(engine, body):
            body(Step(0, 0), STEPS - 1)
            with engine.Fori(0, STEPS // 2 - 2) as i:
                body(Step(i, 1), 3)
                body(Step(i, 1).after(1), 3)
            for n in range(STEPS - 3, STEPS):
                body(Step(n // 2, n % 2), STEPS - 1 - n)

        LAST = Step(STEPS // 2 - 1, 1)

        def y_banks(to_come):
            return pair_yT_r if to_come else pair_gx_attn

        def flat(t):
            return t[:, :, :].rearrange("p k c -> p (k c)")

        def pair(t, h):
            return t[:, 2 * h:2 * h + 2, :].rearrange("p k c -> p (k c)")

        block = ctx.enter_context(nc.Block())

        @block.sync
        def _(sp):
            def load(step):
                if not starts(step, 2):
                    sp.wait_ge(s_dot, step.after(-2).count())
                    sp.wait_ge(s_gx, step.after(-2).count())
                    sp.wait_ge(s_z1, step.after(-2).count(2))
                sp.dma_start(x_tok[step.b][:, :, :], x_steps[step.b, step.j]).then_inc(s_x[step.b], 16)

            def store(step):
                sp.wait_ge(s_out, step.count())
                sp.dma_start(out_steps[step.b, step.j], out_tok[step.b][:, :, :]).then_inc(s_stored[step.b], 16)

            def body(step, to_come):
                if to_come >= 3:
                    load(step.after(3))
                if not starts(step, 1):
                    store(step.after(-1))

            for b in range(2):
                sp.sem_inc(s_stored[b], 16)
            for h in range(2):
                sp.dma_start(x_tok[0][:, 2 * h:2 * h + 2, :], x_steps[0, 0][:, 2 * h:2 * h + 2, :]).then_inc(s_x_first[h], 16)
            sp.dma_start(wout[:, :, :], rows(WoutT)).then_inc(s_wout, 16)
            load(Step(0, 1))
            sp.dma_start(wk[:, :, :], rows(WkT)).then_inc(s_wk, 16)
            sp.dma_start(wv[:, :, :], rows(WvT)).then_inc(s_wv, 16)
            sp.dma_start(wr[:, :, :], rows(WrT)).then_inc(s_wr, 16)
            load(Step(1, 0))
            all_steps(sp, body)
            sp.wait_ge(s_last_dve, 1)
            sp.dma_start(out_steps[LAST.b, LAST.j][:, 2:4, :], out_last[:, 2:4, :]).then_inc(s_last_stored[1], 16)
            sp.wait_ge(s_stored[0], 16 * (STEPS // 2 + 1))
            sp.wait_ge(s_stored[1], 16 * (STEPS // 2))
            for h in range(2):
                sp.wait_ge(s_last_stored[h], 16)

        @block.gpsimd
        def _(pool):
            gp = nc.gpsimd
            gp.memset(ident[:, :], 0.0).then_inc(s_const, 1)
            pool.wait_ge(s_const, 1)
            gp.affine_select(out=ident[:, :], in_=ident[:, :], compare_op=ALU.not_equal, fill=1.0, base=0,
                             pattern=[[-1, P]], channel_multiplier=1).then_inc(s_ident, 1)
            for tile, value in ((minus_half, -0.5), (minus_one, -1.0), (eps, EPS)):
                gp.memset(tile[:, :], value).then_inc(s_const, 1)
            pool.wait_ge(s_const, 4)

            def split_mixed(step):
                for h in range(HALVES):
                    pool.wait_ge(s_mixed_hi, step.count(2, h + 1))
                    gp.tensor_tensor(mixed_lo[:, h, :], mixed[:, 0, h, :], mixed_hi[:, h, :].bitcast(F32),
                                     ALU.subtract).then_inc(s_mixed_lo, 1)

            def weight_low(w, w_hi, w_lo, s_high, s_low):
                pool.wait_ge(s_high, 1)
                gp.tensor_tensor(flat(w_lo), flat(w), flat(w_hi).bitcast(F32), ALU.subtract).then_inc(s_low, 1)

            def split_hidden(step):
                for h in range(HALVES):
                    pool.wait_ge(s_hidden_hi, step.count(2, h + 1))
                    gp.tensor_tensor(hidden_lo[step.b][:, h, :], hidden[step.b][:, h, :], hidden_hi[step.b][:, h, :].bitcast(F32),
                                     ALU.subtract).then_inc(s_hidden_lo, 1)

            def scale_and_offset(n, s_small, s_moments, step):
                pool.wait_ge(s_moments, step.count())
                gp.tensor_tensor(norm[:, n, 0, :], moments[:, n, :, 1], eps[:, :], ALU.add).then_inc(s_small, 1)
                gp.tensor_tensor(norm[:, n, 1, :], moments[:, n, :, 0], minus_one[:, :], ALU.mult).then_inc(s_small, 1)
                pool.wait_ge(s_small, step.count(4, 2))
                gp.tensor_tensor(norm[:, n, 2, :], norm[:, n, 0, :], minus_half[:, :], ALU.pow).then_inc(s_small, 1)
                pool.wait_ge(s_small, step.count(4, 3))
                gp.tensor_tensor(norm[:, n, 3, :], norm[:, n, 1, :], norm[:, n, 2, :], ALU.mult).then_inc(s_small, 1)

            def residual2(step):
                for h in range(2):
                    pool.wait_ge(s_rv, step.count(2, h + 1))
                    gp.tensor_tensor(pair(z2[step.b], h), pair(rv, h), pair(y_tok[step.b], h), ALU.add).then_inc(s_z2, 1)

            def norm2(step):
                if not starts(step, 2):
                    pool.wait_ge(s_stored[step.b], step.j * 16 + 16)
                pool.wait_ge(s_ln2, step.count(4, 4))
                gp.tensor_tensor(settled_pool[:, :], norm[:, 1, 3, 0:1], norm[:, 1, 2, 0:1], ALU.mult)
                for k in range(TILES):
                    last = gp.tensor_scalar(out_tok[step.b][:, k, :], z2[step.b][:, k, :], norm[:, 1, 2, k:k + 1],
                                            norm[:, 1, 3, k:k + 1], ALU.mult, ALU.add)
                last.then_inc(s_out, 1)

            def body(step, to_come):
                if to_come >= 1:
                    split_mixed(step)
                if not starts(step, 1):
                    residual2(step.after(-1))
                if to_come >= 1:
                    scale_and_offset(0, s_ln1, s_mom1, step.after(1))
                if to_come >= 2:
                    split_hidden(step.after(2))
                if not starts(step, 1):
                    scale_and_offset(1, s_ln2, s_mom2, step.after(-1))
                    norm2(step.after(-1))

            weight_low(wout, wout_hi, wout_lo, s_wout_hi, s_wout_lo)
            weight_low(wk, wk_hi, wk_lo, s_wk_hi, s_wk_lo)
            weight_low(wv, wv_hi, wv_lo, s_wv_hi, s_wv_lo)
            scale_and_offset(0, s_ln1, s_mom1, Step(0, 0))
            all_steps(pool, body)
            scale_and_offset(1, s_ln2, s_mom2, LAST)

        @block.scalar
        def _(act):
            sc = nc.scalar
            sc.preload_act_table(ACT.Sigmoid)
            act.dma_start(wg_rows[:, :], Wg.to_broadcast([P, C])).then_inc(s_gate_w, 16)
            act.dma_start(bg_col[:, :], bg.rearrange("(a n) -> a n", a=1).to_broadcast([P, 1])).then_inc(s_gate_w, 16)
            for row in (0, LO_ROW):
                act.dma_start(bout_row[row:row + 1, :], bout.rearrange("(a n) -> a n", a=1)).then_inc(s_bout, 16)
            act.dma_start(mu[:, :, :], mus).then_inc(s_mu, 16)

            def gates(step):
                b = step.b
                act.wait_ge(s_dot, step.count())
                if not starts(step, 2):
                    act.wait_ge(s_decay_t, step.after(-2).count())
                    act.wait_ge(s_gx_t, step.after(-2).count(2))
                sc.activation(gate[b][:, 1, :], gate[b][:, 0, :], ACT.Sigmoid, bias=bg_col[:, 0:1]).then_inc(s_gate, 1)
                act.wait_ge(s_gate, step.count())
                sc.activation(gate[b][:, 2, :], gate[b][:, 1, :], ACT.Identity, scale=-1.0, bias=1.0).then_inc(s_one_minus, 1)

            def gated(step):
                b = step.b
                for k in range(TILES):
                    last = sc.activation(gated_x[b][:, k, :], x_tok[b][:, k, :], ACT.Copy, scale=gate[b][:, 1, k:k + 1])
                last.then_inc(s_gx, 1)

            def copy_decay(step):
                b = step.b
                act.wait_ge(s_decay_t, step.count())
                if not starts(step, 2):
                    act.wait_ge(s_scan, step.after(-2).count(2))
                sc.activation(decay[b][:, :], decay_ps[b][:, :], ACT.Copy).then_inc(s_decay, 1)

            def shift(step, banks):
                b = step.b
                w = shifted[b]
                if not starts(step, 2):
                    act.wait_ge(s_mix_r, step.after(-2).count(2))
                sc.activation(w[:, :, :, 0:1], w[:, :, :, GROUP:GROUP + 1], ACT.Copy).then_inc(s_carry, 1)
                act.wait_ge(s_carry, step.count())
                for h in range(HALVES):
                    act.wait_ge(s_yT, step.count(2, h + 1))
                    for n in range(2):
                        last = sc.activation(w[:, n, h, 1:GROUP + 1], banks[h][:, :], ACT.Copy,
                                             scale=one_minus_mu[:, n, h:h + 1])
                    last.then_inc(s_shift, 1)

            def mixed_high(step, h):
                act.wait_ge(s_mix_k, step.count(2, h + 1))
                sc.activation(mixed_hi[:, h, :], mixed[:, 0, h, :], ACT.Copy).then_inc(s_mixed_hi, 1)

            def weight_high(w, w_hi, s_loaded, s_high):
                act.wait_ge(s_loaded, 16)
                sc.activation(flat(w_hi), flat(w), ACT.Copy).then_inc(s_high, 1)

            def hidden_high(step):
                for h in range(HALVES):
                    act.wait_ge(s_scan, step.count(2, h + 1))
                    sc.activation(hidden_hi[step.b][:, h, :], hidden[step.b][:, h, :], ACT.Copy).then_inc(s_hidden_hi, 1)

            def norm1(step, tiles=range(TILES)):
                act.wait_ge(s_ln1, step.count(4))
                for k in tiles:
                    sc.activation(y_tok[step.b][:, k, :], z1[:, k, :], ACT.Identity, scale=norm[:, 0, 2, k:k + 1],
                                  bias=norm[:, 0, 3, k:k + 1]).then_inc(s_y, 1)

            def relu_squared(step, to_come):
                for h in range(HALVES):
                    act.wait_ge(s_k, step.count(2, h + 1))
                    sc.activation(relu_k[:, h, :], pair_k_v[h][:, :], ACT.Relu).then_inc(s_relu, 1)
                if to_come >= 2:
                    copy_decay(step.after(2))
                for h in range(HALVES):
                    act.wait_ge(s_relu, step.count(2, h + 1))
                    sc.activation(k_act[:, h, :], relu_k[:, h, :], ACT.Square).then_inc(s_kact, 1)
                for h in range(HALVES):
                    act.wait_ge(s_kact, step.count(2, h + 1))
                    sc.activation(k_hi[:, h, :], k_act[:, h, :], ACT.Copy).then_inc(s_k_hi, 1)

            def r_sigmoid(step):
                for h in range(2):
                    act.wait_ge(s_r, step.count(2, h + 1))
                    sc.activation(pair(r_gate, h), pair_yT_r[h][:, :], ACT.Sigmoid).then_inc(s_sig, 1)

            def body(step, to_come):
                shift(step, y_banks(to_come))
                mixed_high(step, 0)
                if to_come >= 2:
                    gates(step.after(2))
                mixed_high(step, 1)
                if to_come >= 2:
                    gated(step.after(2))
                relu_squared(step, to_come)
                if to_come == 1:
                    norm1(step.after(1), (0, 1))
                if to_come >= 2:
                    hidden_high(step.after(2))
                r_sigmoid(step)
                if to_come >= 2:
                    norm1(step.after(1))

            act.wait_ge(s_gate_w, 32)
            gates(Step(0, 0))
            weight_high(wout, wout_hi, s_wout, s_wout_hi)
            copy_decay(Step(0, 0))
            hidden_high(Step(0, 0))
            weight_high(wk, wk_hi, s_wk, s_wk_hi)
            gates(Step(0, 1))
            gated(Step(0, 1))
            copy_decay(Step(0, 1))
            weight_high(wv, wv_hi, s_wv, s_wv_hi)
            hidden_high(Step(0, 1))
            norm1(Step(0, 0), (0, 1))
            act.wait_ge(s_omm, 1)
            act.wait_ge(s_zeros, 4)
            all_steps(act, body)
            act.wait_ge(s_ln2, LAST.count(4))
            for k in (0, 1):
                last = sc.activation(out_last[:, k, :], z2[LAST.b][:, k, :], ACT.Identity,
                                     scale=norm[:, 1, 2, k:k + 1], bias=norm[:, 1, 3, k:k + 1])
            last.then_inc(s_last_act, 1)
            act.wait_ge(s_last_act, 1)
            act.dma_start(out_steps[LAST.b, LAST.j][:, 0:2, :], out_last[:, 0:2, :]).then_inc(s_last_stored[0], 16)

        @block.vector
        def _(dve):
            v = nc.vector

            def gate_dot(step):
                b = step.b
                if not starts(step, 1):
                    dve.wait_ge(s_x[b], (step.j + b) * 16)
                if not starts(step, 2):
                    dve.wait_ge(s_gate, step.after(-2).count())
                for k in range(TILES):
                    if starts(step, 1) and k % 2 == 0:
                        dve.wait_ge(s_x_first[k // 2], 16)
                    last = v.tensor_tensor_reduce(out=dot_terms[:, b, k, :], in0=x_tok[b][:, k, :], in1=wg_rows[:, :],
                                                  scale=1.0, scalar=0.0, op0=ALU.mult, op1=ALU.add,
                                                  accum_out=gate[b][:, 0, k:k + 1])
                last.then_inc(s_dot, 1)

            def scan(step):
                b = step.b
                dve.wait_ge(s_decay, step.count())
                if not starts(step, 2):
                    dve.wait_ge(s_scan, step.after(-2).count(2))
                    dve.wait_ge(s_hidden_hi, step.after(-2).count(2))
                    dve.wait_ge(s_hidden_lo, step.after(-2).count(2))
                for h in range(HALVES):
                    dve.wait_ge(s_gx_t, step.count(2, h + 1))
                    v.tensor_tensor_scan(hidden[b][:, h, :], decay[b][:, :], pair_gx_attn[h][:, :],
                                         hidden[b][:, h, GROUP - 1:GROUP], ALU.mult, ALU.add).then_inc(s_scan, 1)

            def tile_stats(n, z, s_ready, s_st, s_mom, step):
                for k in range(TILES):
                    if k % 2 == 0:
                        dve.wait_ge(s_ready, step.count(2, k // 2 + 1))
                    last = v.bn_stats(stats[:, n, k, :], z[:, k, :])
                last.then_inc(s_st, 1)
                dve.wait_ge(s_st, step.count())
                v.tensor_copy(settled_dve[:, :], stats[:, n, 0, 0:1])
                for k in range(TILES):
                    last = v.bn_aggr(moments[:, n, k, :], stats[:, n, k, :])
                last.then_inc(s_mom, 1)

            def residual1(step, banks=pair_gx_attn):
                for h in range(2):
                    dve.wait_ge(s_attn, step.count(2, h + 1))
                    v.tensor_tensor(pair(z1, h), banks[h][:, :], pair(x_tok[step.b], h), ALU.add).then_inc(s_z1, 1)

            def split_k(step, h):
                dve.wait_ge(s_k_hi, step.count(2, h + 1))
                v.tensor_tensor(k_lo[:, h, :], k_act[:, h, :], k_hi[:, h, :].bitcast(F32), ALU.subtract).then_inc(s_k_lo, 1)

            def mix(step, banks, n, h):
                dve.wait_ge(s_shift, step.count(2, h + 1))
                v.scalar_tensor_tensor(out=mixed[:, n, h, :], in0=banks[h][:, :], scalar=mu[:, n, h:h + 1],
                                       in1=shifted[step.b][:, n, h, 0:GROUP], op0=ALU.mult,
                                       op1=ALU.add).then_inc((s_mix_k, s_mix_r)[n], 1)

            def split_mixed(step, h):
                dve.wait_ge(s_mixed_hi, step.count(2, h + 1))
                v.tensor_tensor(mixed_lo[:, h, :], mixed[:, 0, h, :], mixed_hi[:, h, :].bitcast(F32),
                                ALU.subtract).then_inc(s_mixed_lo, 1)

            def norm1(step, tiles):
                dve.wait_ge(s_ln1, step.count(4))
                for k in tiles:
                    v.tensor_scalar(y_tok[step.b][:, k, :], z1[:, k, :], norm[:, 0, 2, k:k + 1], norm[:, 0, 3, k:k + 1],
                                    ALU.mult, ALU.add).then_inc(s_y, 1)

            def gate_v(step, h):
                dve.wait_ge(s_v, step.count(2, h + 1))
                dve.wait_ge(s_sig, step.count(2, h + 1))
                v.tensor_tensor(pair(rv, h), pair_k_v[h][:, :], pair(r_gate, h), ALU.mult).then_inc(s_rv, 1)

            def split_hidden(step):
                b = step.b
                for h in range(HALVES):
                    dve.wait_ge(s_hidden_hi, step.count(2, h + 1))
                    v.tensor_tensor(hidden_lo[b][:, h, :], hidden[b][:, h, :], hidden_hi[b][:, h, :].bitcast(F32),
                                    ALU.subtract).then_inc(s_hidden_lo, 1)

            def body(step, to_come):
                last = to_come == 0
                if not last:
                    for h in range(HALVES):
                        for n in range(2):
                            mix(step, y_banks(to_come), n, h)
                    residual1(step.after(1))
                    tile_stats(0, z1, s_z1, s_st1, s_mom1, step.after(1))
                if to_come >= 2:
                    scan(step.after(2))
                split_k(step, 0)
                split_k(step, 1)
                if to_come == 1:
                    norm1(step.after(1), (2, 3))
                if not starts(step, 1):
                    stats2(step.after(-1))
                for h in range(2):
                    if to_come == 1:
                        mix(step.after(1), y_banks(0), 0, h)
                    gate_v(step, h)
                if to_come == 1:
                    for h in range(HALVES):
                        split_mixed(step.after(1), h)
                    for h in range(HALVES):
                        mix(step.after(1), y_banks(0), 1, h)
                if to_come >= 3:
                    gate_dot(step.after(3))

            def stats2(step):
                tile_stats(1, z2[step.b], s_z2, s_st2, s_mom2, step)

            v.memset(bout_parts[:, :].bitcast(F32), 0.0).then_inc(s_bias_zero, 1)
            v.memset(ones[:, :].bitcast(F32), 1.0).then_inc(s_bias_zero, 1)
            for b in range(2):
                v.memset(hidden[b][:, :, GROUP - 1:GROUP], 0.0).then_inc(s_zeros, 1)
                v.memset(shifted[b][:, :, :, GROUP:GROUP + 1], 0.0).then_inc(s_zeros, 1)
            dve.wait_ge(s_gate_w, 32)
            gate_dot(Step(0, 0))
            dve.wait_ge(s_gate, 1)
            for k in range(TILES):
                last = v.tensor_scalar(gated_x[0][:, k, :], x_tok[0][:, k, :], gate[0][:, 1, k:k + 1], None, ALU.mult)
            last.then_inc(s_gx, 1)
            dve.wait_ge(s_bout, 16 * 2)
            dve.wait_ge(s_bias_zero, 2)
            v.tensor_copy(bout_parts[0:1, :], bout_row[0:1, :]).then_inc(s_bias, 1)
            v.tensor_copy(bout_hi[LO_ROW:LO_ROW + 1, :], bout_row[LO_ROW:LO_ROW + 1, :]).then_inc(s_bias_hi, 1)
            dve.wait_ge(s_bias_hi, 1)
            v.tensor_tensor(bout_parts[LO_ROW:LO_ROW + 1, :], bout_row[LO_ROW:LO_ROW + 1, :],
                            bout_hi[LO_ROW:LO_ROW + 1, :].bitcast(F32), ALU.subtract).then_inc(s_bias, 1)
            dve.wait_ge(s_zeros, 4)
            scan(Step(0, 0))
            split_hidden(Step(0, 0))
            gate_dot(Step(0, 1))
            dve.wait_ge(s_mu, 16)
            v.tensor_scalar(one_minus_mu[:, :, :], mu[:, :, :], -1.0, 1.0, ALU.mult, ALU.add).then_inc(s_omm, 1)
            residual1(Step(0, 0), pair_k_v)
            tile_stats(0, z1, s_z1, s_st1, s_mom1, Step(0, 0))
            scan(Step(0, 1))
            norm1(Step(0, 0), (2, 3))
            split_hidden(Step(0, 1))
            gate_dot(Step(1, 0))
            all_steps(dve, body)
            for h in range(2):
                dve.wait_ge(s_rv, LAST.count(2, h + 1))
                v.tensor_tensor(pair(z2[LAST.b], h), pair(rv, h), pair(y_tok[LAST.b], h), ALU.add).then_inc(s_z2, 1)
            dve.wait_ge(s_ln2, LAST.after(-1).count(4, 2))
            tile_stats(1, z2[LAST.b], s_z2, s_st2, s_mom2, LAST)
            dve.wait_ge(s_ln2, LAST.count(4))
            for k in (2, 3):
                last = v.tensor_scalar(out_last[:, k, :], z2[LAST.b][:, k, :], norm[:, 1, 2, k:k + 1],
                                       norm[:, 1, 3, k:k + 1], ALU.mult, ALU.add)
            last.then_inc(s_last_dve, 1)

        @block.tensor
        def _(pe):
            t = nc.tensor

            def transpose_gated(step):
                b = step.b
                pe.wait_ge(s_one_minus, step.count())
                if not starts(step, 2):
                    pe.wait_ge(s_decay, step.after(-2).count())
                for k in range(TILES):
                    last = t.transpose(decay_ps[b][:, k * P:(k + 1) * P],
                                       gate[b][:, 2, k:k + 1].to_broadcast([P, P]), ident[:, :])
                last.then_inc(s_decay_t, 1)
                pe.wait_ge(s_gx, step.count())
                if not starts(step, 2):
                    pe.wait_ge(s_z1, step.after(-1).count(2))
                if not starts(step, 1) and starts(step, 2):
                    pe.wait_ge(s_scan, 2)
                for h in range(HALVES):
                    for k in range(TILES):
                        last = t.transpose(pair_gx_attn[h][:, k * P:(k + 1) * P],
                                           gated_x[b][:, k, h * P:(h + 1) * P], ident[:, :])
                    last.then_inc(s_gx_t, 1)

            def token_product(banks, lhs, w, s_done):
                for h in range(2):
                    for k in (2 * h, 2 * h + 1):
                        for c in range(HALVES):
                            last = t.matmul(banks[h][:, (k % 2) * C:(k % 2 + 1) * C], lhs[:, c, k * P:(k + 1) * P],
                                            w[:, c, :], start=(c == 0), stop=(c == HALVES - 1))
                    last.then_inc(s_done, 1)

            def split_token_product(banks, x_hi, x_lo, w_hi, w_lo, s_lo, lo_count, s_done, bias=False):
                for h in range(2):
                    for k in (2 * h, 2 * h + 1):
                        columns = banks[h][:, (k % 2) * C:(k % 2 + 1) * C]
                        if bias:
                            t.matmul(columns, ones[:, :], bout_parts[:, :], start=True, stop=False)
                        for n, (x_part, w_part, c) in enumerate(
                                [(x, w, c) for x, w in ((x_hi, w_lo), (x_hi, w_hi), (x_lo, w_hi)) for c in range(HALVES)]):
                            if k == 0 and n == 2 * HALVES:
                                pe.wait_ge(s_lo, lo_count)
                            last = t.matmul(columns, x_part[:, c, k * P:(k + 1) * P], w_part[:, c, :],
                                            start=(n == 0 and not bias), stop=(n == 3 * HALVES - 1))
                    last.then_inc(s_done, 1)

            def attn(step, banks=pair_gx_attn):
                pe.wait_ge(s_hidden_hi, step.count(2))
                split_token_product(banks, hidden_hi[step.b], hidden_lo[step.b], wout_hi, wout_lo,
                                    s_hidden_lo, step.count(2), s_attn, bias=True)

            def transpose_y(step, banks):
                pe.wait_ge(s_y, step.count(4))
                if banks is pair_yT_r and not starts(step, 1):
                    pe.wait_ge(s_sig, step.after(-1).count(2))
                for h in range(HALVES):
                    for k in range(TILES):
                        last = t.transpose(banks[h][:, k * P:(k + 1) * P],
                                           y_tok[step.b][:, k, h * P:(h + 1) * P], ident[:, :])
                    last.then_inc(s_yT, 1)

            def k_product(step):
                if starts(step, 1):
                    pe.wait_ge(s_wk_hi, 1)
                    pe.wait_ge(s_wk_lo, 1)
                else:
                    pe.wait_ge(s_rv, step.after(-1).count(2))
                for c in range(HALVES):
                    pe.wait_ge(s_mixed_hi, step.count(2, c + 1))
                    for h in range(HALVES):
                        for w_part in (wk_lo, wk_hi):
                            t.matmul(pair_k_v[h][:, :], w_part[:, c, h * P:(h + 1) * P], mixed_hi[:, c, :],
                                     start=(c == 0 and w_part is wk_lo), stop=False)
                pe.wait_ge(s_mixed_lo, step.count(2))
                for h in range(HALVES):
                    for c in range(HALVES):
                        last = t.matmul(pair_k_v[h][:, :], wk_hi[:, c, h * P:(h + 1) * P], mixed_lo[:, c, :],
                                        start=False, stop=(c == HALVES - 1))
                    last.then_inc(s_k, 1)

            def r_product(step):
                if starts(step, 1):
                    pe.wait_ge(s_wr, 16)
                pe.wait_ge(s_mix_r, step.count(2))
                token_product(pair_yT_r, mixed[:, 1], wr, s_r)

            def v_product(step):
                if starts(step, 1):
                    pe.wait_ge(s_wv_hi, 1)
                    pe.wait_ge(s_wv_lo, 1)
                pe.wait_ge(s_k_hi, step.count(2))
                split_token_product(pair_k_v, k_hi, k_lo, wv_hi, wv_lo, s_k_lo, step.count(2), s_v)

            def body(step, to_come):
                if to_come >= 1:
                    transpose_y(step, pair_yT_r)
                    attn(step.after(1))
                k_product(step)
                if to_come >= 2:
                    transpose_gated(step.after(2))
                r_product(step)
                if to_come == 1:
                    transpose_y(step.after(1), y_banks(0))
                v_product(step)

            def keep_warm(n):
                for _ in range(n):
                    t.matmul(pair_yT_r[0][:, 0:P], ident[:, :], ident[:, :], start=True, stop=True)

            pe.wait_ge(s_ident, 1)
            keep_warm(WARM_UP[0])
            transpose_gated(Step(0, 0))
            keep_warm(WARM_UP[1])
            pe.wait_ge(s_wout_hi, 1)
            pe.wait_ge(s_wout_lo, 1)
            pe.wait_ge(s_bias, 2)
            attn(Step(0, 0), pair_k_v)
            transpose_gated(Step(0, 1))
            keep_warm(WARM_UP[2])
            all_steps(pe, body)


def kernel(L0_attn_x, L0_attn_Wg, L0_attn_bg, L0_attn_Wout, L0_attn_bout, L0_ffn_W_r, L0_ffn_W_k, L0_ffn_W_v,
           L0_ffn_mu_r, L0_ffn_mu_k):
    import numpy as np
    import concourse.bacc as bacc
    from concourse.bass_utils import run_bass_kernel_spmd

    nc = bacc.Bacc("TRN2", target_bir_lowering=False, num_devices=1)
    arrays = {
        "x": L0_attn_x, "Wg": L0_attn_Wg, "bg": L0_attn_bg, "WoutT": np.transpose(L0_attn_Wout), "bout": L0_attn_bout,
        "WrT": np.transpose(L0_ffn_W_r), "WkT": np.transpose(L0_ffn_W_k), "WvT": np.transpose(L0_ffn_W_v),
        "mus": np.transpose(np.stack([L0_ffn_mu_k, L0_ffn_mu_r]).reshape(2, -1, P), (2, 0, 1)),
    }
    arrays = {n: np.ascontiguousarray(a) for n, a in arrays.items()}
    ins = [nc.dram_tensor(n, a.shape, mybir.dt.from_np(a.dtype), kind="ExternalInput").ap() for n, a in arrays.items()]
    out = nc.dram_tensor("out", arrays["x"].shape, F32, kind="ExternalOutput").ap()
    build(nc, *ins, out)
    ran = run_bass_kernel_spmd(nc, [arrays], core_ids=[0])
    return ran.results[0]["out"]
```

```python
from contextlib import ExitStack

import concourse.bass as bass
from concourse import mybir

P = 128
GROUP = 512
TILES = GROUP // P
ALU = mybir.AluOpType
ACT = mybir.ActivationFunctionType
F32 = mybir.dt.float32
F32R = mybir.dt.float32r
EPS = 1e-5
LO_ROW = 32
WARM_UP = (9, 6, 10)


class Step:

    def __init__(self, j, b):
        self.j, self.b = j, b

    def after(self, n=1):
        return Step(self.j + (self.b + n) // 2, (self.b + n) % 2)

    def count(self, each=1, part=None):
        return (self.j * 2 + self.b) * each + (each if part is None else part)


def build(nc, x, Wg, bg, WoutT, bout, WrT, WkT, WvT, mus, out):
    B, T, C = x.shape
    HALVES = C // P
    STEPS = B * T // GROUP
    assert B == 2 and C == 2 * P and T % GROUP == 0 and STEPS >= 6

    x_steps = x.rearrange("b (j k p) c -> b j p k c", p=P, k=TILES)
    out_steps = out.rearrange("b (j k p) c -> b j p k c", p=P, k=TILES)

    def rows(w):
        return w.rearrange("(h p) n -> p h n", p=P)

    with ExitStack() as ctx:
        def sb(name, shape, dtype=F32):
            return ctx.enter_context(nc.sbuf_tensor(name, shape, dtype))

        def psum(name, shape):
            return ctx.enter_context(nc.psum_tensor(name, shape, F32))

        def sem(name):
            return ctx.enter_context(nc.semaphore(name))

        wout = sb("wout", [P, HALVES, C])
        wk = sb("wk", [P, HALVES, C])
        wr = sb("wr", [P, HALVES, C])
        wv = sb("wv", [P, HALVES, C])
        wg_rows = sb("wg_rows", [P, C])
        wout_hi = sb("wout_hi", [P, HALVES, C], F32R)
        wout_lo = sb("wout_lo", [P, HALVES, C], F32R)
        wk_hi = sb("wk_hi", [P, HALVES, C], F32R)
        wk_lo = sb("wk_lo", [P, HALVES, C], F32R)
        wv_hi = sb("wv_hi", [P, HALVES, C], F32R)
        wv_lo = sb("wv_lo", [P, HALVES, C], F32R)
        bout_row = sb("bout_row", [P, C])
        bout_parts = sb("bout_parts", [P, C], F32R)
        ones = sb("ones", [P, P], F32R)
        bg_col = sb("bg_col", [P, 1])
        mu = sb("mu", [P, 2, HALVES])
        one_minus_mu = sb("one_minus_mu", [P, 2, HALVES])
        ident = sb("ident", [P, P])
        minus_half = sb("minus_half", [P, TILES])
        minus_one = sb("minus_one", [P, TILES])
        eps = sb("eps", [P, TILES])
        settled_pool = sb("settled_pool", [P, 1])
        settled_dve = sb("settled_dve", [P, 1])

        x_tok = [sb(f"x_tok{b}", [P, TILES, C]) for b in range(2)]
        gated_x = [sb(f"gated_x{b}", [P, TILES, C]) for b in range(2)]
        gate = [sb(f"gate{b}", [P, 3, TILES]) for b in range(2)]
        decay = [sb(f"decay{b}", [P, GROUP]) for b in range(2)]
        hidden = [sb(f"hidden{b}", [P, HALVES, GROUP]) for b in range(2)]
        y_tok = [sb(f"y_tok{b}", [P, TILES, C]) for b in range(2)]
        shifted = [sb(f"shifted{b}", [P, 2, HALVES, GROUP + 1]) for b in range(2)]
        z2 = [sb(f"z2_{b}", [P, TILES, C]) for b in range(2)]
        z2_last = sb("z2_last", [P, TILES, C])
        out_last = sb("out_last", [P, TILES, C])
        out_tok = [sb(f"out_tok{b}", [P, TILES, C]) for b in range(2)]
        dot_terms = sb("dot_terms", [P, 2, TILES, C])
        z1 = sb("z1", [P, TILES, C])
        stats = sb("stats", [P, 2, TILES, 6])
        moments = sb("moments", [P, 2, TILES, 2])
        norm = sb("norm", [P, 2, 4, TILES])
        norm_last = sb("norm_last", [P, 2, 4, TILES])
        mixed = sb("mixed", [P, 2, HALVES, GROUP])
        mixed_hi = sb("mixed_hi", [P, HALVES, GROUP], F32R)
        mixed_lo = sb("mixed_lo", [P, HALVES, GROUP], F32R)
        hidden_hi = [sb(f"hidden_hi{b}", [P, HALVES, GROUP], F32R) for b in range(2)]
        hidden_lo = [sb(f"hidden_lo{b}", [P, HALVES, GROUP], F32R) for b in range(2)]
        relu_k = sb("relu_k", [P, HALVES, GROUP])
        k_act = sb("k_act", [P, HALVES, GROUP])
        k_hi = sb("k_hi", [P, HALVES, GROUP], F32R)
        k_lo = sb("k_lo", [P, HALVES, GROUP], F32R)
        r_gate = sb("r_gate", [P, TILES, C])
        rv = sb("rv", [P, TILES, C])

        pair_yT_r = [psum(f"pair_yT_r{h}", [P, GROUP]) for h in range(2)]
        pair_gx_attn = [psum(f"pair_gx_attn{h}", [P, GROUP]) for h in range(2)]
        pair_k_v = [psum(f"pair_k_v{h}", [P, GROUP]) for h in range(2)]
        decay_ps = [psum(f"decay_ps{b}", [P, GROUP]) for b in range(2)]

        s_x = [sem(f"s_x{b}") for b in range(2)]
        s_x_first = [sem(f"s_x_first{h}") for h in range(2)]
        s_gate_w = sem("s_gate_w")
        s_bout = sem("s_bout")
        s_wout = sem("s_wout")
        s_mu = sem("s_mu")
        s_wk = sem("s_wk")
        s_wr = sem("s_wr")
        s_wv = sem("s_wv")
        s_ident = sem("s_ident")
        s_const = sem("s_const")
        s_zeros = sem("s_zeros")
        s_omm = sem("s_omm")
        s_bias_zero = sem("s_bias_zero")
        s_bias = sem("s_bias")
        s_ones = sem("s_ones")
        s_wout_hi = sem("s_wout_hi")
        s_wout_lo = sem("s_wout_lo")
        s_wk_hi = sem("s_wk_hi")
        s_wk_lo = sem("s_wk_lo")
        s_wv_hi = sem("s_wv_hi")
        s_wv_lo = sem("s_wv_lo")
        s_dot = sem("s_dot")
        s_gate = sem("s_gate")
        s_one_minus = sem("s_one_minus")
        s_gx = sem("s_gx")
        s_decay_t = sem("s_decay_t")
        s_gx_t = sem("s_gx_t")
        s_decay = sem("s_decay")
        s_scan = sem("s_scan")
        s_hidden_hi = sem("s_hidden_hi")
        s_hidden_lo = sem("s_hidden_lo")
        s_attn = sem("s_attn")
        s_z1 = sem("s_z1")
        s_st1 = sem("s_st1")
        s_mom1 = sem("s_mom1")
        s_ln1 = sem("s_ln1")
        s_y = sem("s_y")
        s_yT = sem("s_yT")
        s_carry = sem("s_carry")
        s_shift = sem("s_shift")
        s_mix_k = sem("s_mix_k")
        s_mix_r = sem("s_mix_r")
        s_mixed_hi = sem("s_mixed_hi")
        s_mixed_lo = [sem(f"s_mixed_lo{h}") for h in range(2)]
        s_k = sem("s_k")
        s_relu = sem("s_relu")
        s_kact = sem("s_kact")
        s_k_hi = sem("s_k_hi")
        s_k_lo = [sem(f"s_k_lo{h}") for h in range(2)]
        s_r = sem("s_r")
        s_sig = sem("s_sig")
        s_v = sem("s_v")
        s_rv = sem("s_rv")
        s_z2 = sem("s_z2")
        s_st2 = sem("s_st2")
        s_mom2 = sem("s_mom2")
        s_ln2 = sem("s_ln2")
        s_out = sem("s_out")
        s_first_gate = [sem("s_first_gate"), s_gate]
        s_first_one_minus = [sem("s_first_one_minus"), s_one_minus]
        s_first_gx = [sem("s_first_gx"), s_gx]
        s_first_mom1 = [sem("s_first_mom1"), s_mom1]
        s_first_ln1 = [sem("s_first_ln1"), s_ln1]
        s_first_hidden_lo = sem("s_first_hidden_lo")
        s_first_decay_t = [sem("s_first_decay_t"), s_decay_t]
        s_first_decay = [sem("s_first_decay"), s_decay]
        s_last_y = [sem(f"s_last_y_{engine}") for engine in ("act", "dve")]
        s_last_yT = sem("s_last_yT")
        s_last_shift = [sem(f"s_last_shift_{n}") for n in ("k", "r")]
        s_last_mixed_lo = sem("s_last_mixed_lo")
        s_last_k_lo = [sem(f"s_last_k_lo{h}") for h in range(2)]
        s_last_mom = [[sem(f"s_last_mom{n}_{h}") for h in range(2)] for n in (1, 2)]
        s_last_norm = [[sem(f"s_last_norm{n}_{h}") for h in range(2)] for n in (1, 2)]
        s_last_out = sem("s_last_out")
        s_last_dve = sem("s_last_dve")
        s_last_stored = [sem(f"s_last_stored{h}") for h in range(2)]
        s_stored = [sem(f"s_stored{b}") for b in range(2)]

        def starts(step, before):
            return isinstance(step.j, int) and 2 * step.j + step.b < before

        def all_steps(engine, body):
            body(Step(0, 0), STEPS - 1)
            with engine.Fori(0, STEPS // 2 - 2) as i:
                body(Step(i, 1), 3)
                body(Step(i, 1).after(1), 3)
            for n in range(STEPS - 3, STEPS - 1):
                body(Step(n // 2, n % 2), STEPS - 1 - n)

        LAST = Step(STEPS // 2 - 1, 1)

        def half_tokens(part):
            return slice(part * GROUP // 2, (part + 1) * GROUP // 2)

        def by_half(bank):
            return bank[:, :].rearrange("p (h t) -> p h t", h=HALVES)

        def flat(t):
            return t[:, :, :].rearrange("p k c -> p (k c)")

        def pair(t, h):
            return t[:, 2 * h:2 * h + 2, :].rearrange("p k c -> p (k c)")

        block = ctx.enter_context(nc.Block())

        @block.sync
        def _(sp):
            def load(step):
                if not starts(step, 2):
                    sp.wait_ge(s_z1, step.after(-2).count(2))
                sp.dma_start(x_tok[step.b][:, :, :], x_steps[step.b, step.j]).then_inc(s_x[step.b], 16)

            def store(step):
                sp.wait_ge(s_out, step.count())
                sp.dma_start(out_steps[step.b, step.j], out_tok[step.b][:, :, :]).then_inc(s_stored[step.b], 16)

            def body(step, to_come):
                if to_come >= 3:
                    load(step.after(3))
                if not starts(step, 1):
                    store(step.after(-1))

            for b in range(2):
                sp.sem_inc(s_stored[b], 16)
            for h in range(2):
                sp.dma_start(x_tok[0][:, 2 * h:2 * h + 2, :], x_steps[0, 0][:, 2 * h:2 * h + 2, :]).then_inc(s_x_first[h], 16)
            sp.dma_start(wout[:, :, :], rows(WoutT)).then_inc(s_wout, 16)
            load(Step(0, 1))
            sp.dma_start(wk[:, :, :], rows(WkT)).then_inc(s_wk, 16)
            sp.dma_start(wv[:, :, :], rows(WvT)).then_inc(s_wv, 16)
            sp.dma_start(wr[:, :, :], rows(WrT)).then_inc(s_wr, 16)
            load(Step(1, 0))
            all_steps(sp, body)
            store(LAST.after(-1))
            for h in range(2):
                sp.wait_ge(s_last_out, 2 + h)
                if h == 1:
                    sp.wait_ge(s_last_dve, 1)
                sp.dma_start(out_steps[LAST.b, LAST.j][:, 2 * h:2 * h + 2, :],
                             out_last[:, 2 * h:2 * h + 2, :]).then_inc(s_last_stored[h], 16)
            sp.wait_ge(s_stored[0], 16 * (STEPS // 2 + 1))
            sp.wait_ge(s_stored[1], 16 * (STEPS // 2))
            for h in range(2):
                sp.wait_ge(s_last_stored[h], 16)

        @block.gpsimd
        def _(pool):
            gp = nc.gpsimd
            gp.memset(ident[:, :], 0.0).then_inc(s_const, 1)
            pool.wait_ge(s_const, 1)
            gp.affine_select(out=ident[:, :], in_=ident[:, :], compare_op=ALU.not_equal, fill=1.0, base=0,
                             pattern=[[-1, P]], channel_multiplier=1).then_inc(s_ident, 1)
            for tile, value in ((minus_half, -0.5), (minus_one, -1.0), (eps, EPS)):
                gp.memset(tile[:, :], value).then_inc(s_const, 1)
            pool.wait_ge(s_const, 4)

            def split_mixed(step, h):
                pool.wait_ge(s_mixed_hi, step.count(2, h + 1))
                gp.tensor_tensor(mixed_lo[:, h, :], mixed[:, 0, h, :], mixed_hi[:, h, :].bitcast(F32),
                                 ALU.subtract).then_inc(s_mixed_lo[h], 1)

            def weight_low(w, w_hi, w_lo, s_high, s_low):
                pool.wait_ge(s_high, 1)
                gp.tensor_tensor(flat(w_lo), flat(w), flat(w_hi).bitcast(F32), ALU.subtract).then_inc(s_low, 1)

            def split_hidden(step):
                for h in range(HALVES):
                    pool.wait_ge(s_hidden_hi, step.count(2, h + 1))
                    gp.tensor_tensor(hidden_lo[step.b][:, h, :], hidden[step.b][:, h, :], hidden_hi[step.b][:, h, :].bitcast(F32),
                                     ALU.subtract).then_inc(s_hidden_lo, 1)

            def scale_and_offset(n, s_small, s_moments, step):
                pool.wait_ge(s_moments, step.count())
                gp.tensor_tensor(norm[:, n, 0, :], moments[:, n, :, 1], eps[:, :], ALU.add).then_inc(s_small, 1)
                gp.tensor_tensor(norm[:, n, 1, :], moments[:, n, :, 0], minus_one[:, :], ALU.mult).then_inc(s_small, 1)
                pool.wait_ge(s_small, step.count(4, 2))
                gp.tensor_tensor(norm[:, n, 2, :], norm[:, n, 0, :], minus_half[:, :], ALU.pow).then_inc(s_small, 1)
                pool.wait_ge(s_small, step.count(4, 3))
                gp.tensor_tensor(norm[:, n, 3, :], norm[:, n, 1, :], norm[:, n, 2, :], ALU.mult).then_inc(s_small, 1)

            def split_k(step):
                pool.wait_ge(s_k_hi, step.count(2))
                gp.tensor_tensor(k_lo[:, 1, :], k_act[:, 1, :], k_hi[:, 1, :].bitcast(F32), ALU.subtract).then_inc(s_k_lo[1], 1)

            def scale_and_offset_by_halves(n, norm_n, moments_done, small):
                for part in range(2):
                    tiles = slice(2 * part, 2 * part + 2)
                    s_small = small[part]
                    pool.wait_ge(moments_done[part], 1)
                    gp.tensor_tensor(norm_n[:, 0, tiles], moments[:, n, tiles, 1], eps[:, tiles], ALU.add).then_inc(s_small, 1)
                    gp.tensor_tensor(norm_n[:, 1, tiles], moments[:, n, tiles, 0], minus_one[:, tiles], ALU.mult).then_inc(s_small, 1)
                    pool.wait_ge(s_small, 2)
                    gp.tensor_tensor(norm_n[:, 2, tiles], norm_n[:, 0, tiles], minus_half[:, tiles], ALU.pow).then_inc(s_small, 1)
                    pool.wait_ge(s_small, 3)
                    gp.tensor_tensor(norm_n[:, 3, tiles], norm_n[:, 1, tiles], norm_n[:, 2, tiles], ALU.mult).then_inc(s_small, 1)

            def residual2(step):
                for h in range(2):
                    pool.wait_ge(s_rv, step.count(2, h + 1))
                    gp.tensor_tensor(pair(z2[step.b], h), pair(rv, h), pair(y_tok[step.b], h), ALU.add).then_inc(s_z2, 1)

            def norm2(step):
                if not starts(step, 2):
                    pool.wait_ge(s_stored[step.b], step.j * 16 + 16)
                pool.wait_ge(s_ln2, step.count(4, 4))
                gp.tensor_tensor(settled_pool[:, :], norm[:, 1, 3, 0:1], norm[:, 1, 2, 0:1], ALU.mult)
                for k in range(TILES):
                    last = gp.tensor_scalar(out_tok[step.b][:, k, :], z2[step.b][:, k, :], norm[:, 1, 2, k:k + 1],
                                            norm[:, 1, 3, k:k + 1], ALU.mult, ALU.add)
                last.then_inc(s_out, 1)

            def body(step, to_come):
                split_mixed(step, 0)
                if not starts(step, 1):
                    residual2(step.after(-1))
                if to_come >= 2:
                    scale_and_offset(0, s_ln1, s_mom1, step.after(1))
                if to_come == 3:
                    split_k(step)
                elif to_come == 1:
                    scale_and_offset_by_halves(0, norm_last[:, 0], s_last_mom[0], s_last_norm[0])
                if to_come >= 2:
                    split_hidden(step.after(2))
                if not starts(step, 1):
                    scale_and_offset(1, s_ln2, s_mom2, step.after(-1))
                    norm2(step.after(-1))

            weight_low(wout, wout_hi, wout_lo, s_wout_hi, s_wout_lo)
            pool.wait_ge(s_hidden_hi, 2)
            gp.tensor_tensor(hidden_lo[0][:, :, half_tokens(1)], hidden[0][:, :, half_tokens(1)],
                             hidden_hi[0][:, :, half_tokens(1)].bitcast(F32), ALU.subtract).then_inc(s_hidden_lo, 2)
            weight_low(wk, wk_hi, wk_lo, s_wk_hi, s_wk_lo)
            scale_and_offset_by_halves(0, norm[:, 0], s_first_mom1, s_first_ln1)
            weight_low(wv, wv_hi, wv_lo, s_wv_hi, s_wv_lo)
            all_steps(pool, body)
            residual2(LAST.after(-1))
            pool.wait_ge(s_k_hi, LAST.count(2))
            tokens = half_tokens(1)
            gp.tensor_tensor(k_lo[:, :, tokens], k_act[:, :, tokens], k_hi[:, :, tokens].bitcast(F32),
                             ALU.subtract).then_inc(s_last_k_lo[1], 1)
            scale_and_offset(1, s_ln2, s_mom2, LAST.after(-1))
            scale_and_offset_by_halves(1, norm_last[:, 1], s_last_mom[1], s_last_norm[1])

        @block.scalar
        def _(act):
            sc = nc.scalar
            sc.preload_act_table(ACT.Sigmoid)
            act.dma_start(wg_rows[:, :], Wg.to_broadcast([P, C])).then_inc(s_gate_w, 16)
            act.dma_start(bg_col[:, :], bg.rearrange("(a n) -> a n", a=1).to_broadcast([P, 1])).then_inc(s_gate_w, 16)
            act.wait_ge(s_bias_zero, 1)
            for row in (0, LO_ROW):
                act.dma_start(bout_row[row:row + 1, :], bout.rearrange("(a n) -> a n", a=1)).then_inc(s_bout, 16)
            act.dma_start(mu[:, :, :], mus).then_inc(s_mu, 16)

            def gates(step):
                b = step.b
                act.wait_ge(s_dot, step.count(4))
                if not starts(step, 2):
                    act.wait_ge(s_decay_t, step.after(-2).count())
                    act.wait_ge(s_gx_t, step.after(-2).count(2))
                sc.activation(gate[b][:, 1, :], gate[b][:, 0, :], ACT.Sigmoid, bias=bg_col[:, 0:1]).then_inc(s_gate, 1)
                act.wait_ge(s_gate, step.count())
                sc.activation(gate[b][:, 2, :], gate[b][:, 1, :], ACT.Identity, scale=-1.0, bias=1.0).then_inc(s_one_minus, 1)

            def gated(step):
                b = step.b
                for k in range(TILES):
                    last = sc.activation(gated_x[b][:, k, :], x_tok[b][:, k, :], ACT.Copy, scale=gate[b][:, 1, k:k + 1])
                last.then_inc(s_gx, 1)

            def copy_decay(step):
                b = step.b
                act.wait_ge(s_decay_t, step.count())
                if not starts(step, 2):
                    act.wait_ge(s_scan, step.after(-2).count(2))
                sc.activation(decay[b][:, :], decay_ps[b][:, :], ACT.Copy).then_inc(s_decay, 1)

            def carry(step):
                w = shifted[step.b]
                if not starts(step, 2):
                    act.wait_ge(s_mix_r, step.after(-2).count(2))
                sc.activation(w[:, :, :, 0:1], w[:, :, :, GROUP:GROUP + 1], ACT.Copy).then_inc(s_carry, 1)
                act.wait_ge(s_carry, step.count())

            def shift(step):
                w = shifted[step.b]
                carry(step)
                for h in range(HALVES):
                    act.wait_ge(s_yT, step.count(2, h + 1))
                    for n in range(2):
                        last = sc.activation(w[:, n, h, 1:GROUP + 1], pair_yT_r[h][:, :], ACT.Copy,
                                             scale=one_minus_mu[:, n, h:h + 1])
                    last.then_inc(s_shift, 1)

            def mixed_high(step, h):
                act.wait_ge(s_mix_k, step.count(2, h + 1))
                sc.activation(mixed_hi[:, h, :], mixed[:, 0, h, :], ACT.Copy).then_inc(s_mixed_hi, 1)

            def weight_high(w, w_hi, s_loaded, s_high):
                act.wait_ge(s_loaded, 16)
                sc.activation(flat(w_hi), flat(w), ACT.Copy).then_inc(s_high, 1)

            def hidden_high(step, halves=range(HALVES)):
                for h in halves:
                    act.wait_ge(s_scan, step.count(2, h + 1))
                    sc.activation(hidden_hi[step.b][:, h, :], hidden[step.b][:, h, :], ACT.Copy).then_inc(s_hidden_hi, 1)

            def half_norm1(step, part, norm_1, small, s_done):
                k = 2 * part
                act.wait_ge(small[part], 4)
                sc.activation(y_tok[step.b][:, k, :], z1[:, k, :], ACT.Identity, scale=norm_1[:, 2, k:k + 1],
                              bias=norm_1[:, 3, k:k + 1]).then_inc(s_done, 1)

            def norm1(step):
                act.wait_ge(s_ln1, step.count(4))
                for k in range(TILES):
                    sc.activation(y_tok[step.b][:, k, :], z1[:, k, :], ACT.Identity, scale=norm[:, 0, 2, k:k + 1],
                                  bias=norm[:, 0, 3, k:k + 1]).then_inc(s_y, 1)

            def relu_squared(step, to_come):
                for h in range(HALVES):
                    act.wait_ge(s_k, step.count(2, h + 1))
                    sc.activation(relu_k[:, h, :], pair_k_v[h][:, :], ACT.Relu).then_inc(s_relu, 1)
                if to_come >= 2:
                    copy_decay(step.after(2))
                for h in range(HALVES):
                    act.wait_ge(s_relu, step.count(2, h + 1))
                    sc.activation(k_act[:, h, :], relu_k[:, h, :], ACT.Square).then_inc(s_kact, 1)
                if to_come == 1:
                    half_norm1(LAST, 0, norm_last[:, 0], s_last_norm[0], s_last_y[0])
                for h in range(HALVES):
                    act.wait_ge(s_kact, step.count(2, h + 1))
                    sc.activation(k_hi[:, h, :], k_act[:, h, :], ACT.Copy).then_inc(s_k_hi, 1)

            def r_sigmoid(step, banks, h):
                act.wait_ge(s_r, step.count(2, h + 1))
                sc.activation(pair(r_gate, h), banks[h][:, :], ACT.Sigmoid).then_inc(s_sig, 1)

            def body(step, to_come):
                shift(step)
                mixed_high(step, 0)
                if to_come >= 2:
                    gates(step.after(2))
                mixed_high(step, 1)
                if to_come >= 2:
                    gated(step.after(2))
                relu_squared(step, to_come)
                if to_come >= 2:
                    hidden_high(step.after(2))
                    r_sigmoid(step, pair_yT_r, 0)
                    norm1(step.after(1))
                    r_sigmoid(step, pair_yT_r, 1)
                else:
                    half_norm1(LAST, 1, norm_last[:, 0], s_last_norm[0], s_last_y[0])
                    carry(step.after(1))
                    r_sigmoid(step, pair_yT_r, 0)

            def last_shift(n, part):
                act.wait_ge(s_last_yT, part + 1)
                if n == 1:
                    act.wait_ge(s_mix_k, LAST.count(2, part + 1))
                for h in range(HALVES):
                    start = half_tokens(part).start + 1
                    last = sc.activation(shifted[LAST.b][:, n, h, start:start + GROUP // 2],
                                         pair_gx_attn[part][:, half_tokens(h)], ACT.Copy, scale=one_minus_mu[:, n, h:h + 1])
                last.then_inc(s_last_shift[n], 1)

            def norm2(step):
                act.wait_ge(s_stored[step.b], step.j * 16 + 16)
                act.wait_ge(s_ln2, step.count(4))
                for k in range(TILES):
                    last = sc.activation(out_tok[step.b][:, k, :], z2[step.b][:, k, :], ACT.Identity,
                                         scale=norm[:, 1, 2, k:k + 1], bias=norm[:, 1, 3, k:k + 1])
                last.then_inc(s_out, 1)

            def last_mixed_high(part):
                act.wait_ge(s_mix_k, LAST.count(2, part + 1))
                sc.activation(mixed_hi[:, :, half_tokens(part)], mixed[:, 0, :, half_tokens(part)],
                              ACT.Copy).then_inc(s_mixed_hi, 1)

            def last_step():
                last_shift(0, 0)
                last_shift(0, 1)
                r_sigmoid(LAST.after(-1), pair_yT_r, 1)
                last_mixed_high(0)
                last_shift(1, 0)
                last_mixed_high(1)
                last_shift(1, 1)
                for part in range(2):
                    tokens = half_tokens(part)
                    act.wait_ge(s_k, LAST.count(2, part + 1))
                    sc.activation(relu_k[:, :, tokens], by_half(pair_yT_r[part]), ACT.Relu).then_inc(s_relu, 1)
                    act.wait_ge(s_relu, LAST.count(2, part + 1))
                    sc.activation(k_act[:, :, tokens], relu_k[:, :, tokens], ACT.Square).then_inc(s_kact, 1)
                    act.wait_ge(s_kact, LAST.count(2, part + 1))
                    sc.activation(k_hi[:, :, tokens], k_act[:, :, tokens], ACT.Copy).then_inc(s_k_hi, 1)
                for part in range(2):
                    act.wait_ge(s_rv, LAST.after(-1).count(2, part + 1))
                    r_sigmoid(LAST, pair_gx_attn, part)
                norm2(LAST.after(-1))

            def first_gates(part):
                act.wait_ge(s_dot, 2 * (part + 1))
                tiles = slice(2 * part, 2 * part + 2)
                sc.activation(gate[0][:, 1, tiles], gate[0][:, 0, tiles], ACT.Sigmoid, bias=bg_col[:, 0:1]).then_inc(s_first_gate[part], 1)
                act.wait_ge(s_first_gate[part], 1)
                sc.activation(gate[0][:, 2, tiles], gate[0][:, 1, tiles], ACT.Identity, scale=-1.0,
                              bias=1.0).then_inc(s_first_one_minus[part], 1)

            def first_copy_decay(part):
                act.wait_ge(s_first_decay_t[part], 1)
                sc.activation(decay[0][:, half_tokens(part)], decay_ps[part][:, half_tokens(part)],
                              ACT.Copy).then_inc(s_first_decay[part], 1)

            def first_hidden_high(part):
                act.wait_ge(s_scan, part + 1)
                sc.activation(hidden_hi[0][:, :, half_tokens(part)], hidden[0][:, :, half_tokens(part)],
                              ACT.Copy).then_inc(s_hidden_hi, 1)

            act.wait_ge(s_gate_w, 32)
            first_gates(0)
            first_gates(1)
            act.wait_ge(s_bout, 16 * 2)
            sc.activation(bout_parts[:, :], bout_row[:, :], ACT.Copy).then_inc(s_bias, 1)
            first_copy_decay(0)
            weight_high(wout, wout_hi, s_wout, s_wout_hi)
            first_copy_decay(1)
            first_hidden_high(0)
            first_hidden_high(1)
            weight_high(wk, wk_hi, s_wk, s_wk_hi)
            weight_high(wv, wv_hi, s_wv, s_wv_hi)
            gates(Step(0, 1))
            gated(Step(0, 1))
            copy_decay(Step(0, 1))
            half_norm1(Step(0, 0), 0, norm[:, 0], s_first_ln1, s_y)
            hidden_high(Step(0, 1), (0,))
            half_norm1(Step(0, 0), 1, norm[:, 0], s_first_ln1, s_y)
            hidden_high(Step(0, 1), (1,))
            act.wait_ge(s_omm, 1)
            act.wait_ge(s_zeros, 4)
            all_steps(act, body)
            last_step()
            for k in range(TILES - 1):
                if k % 2 == 0:
                    act.wait_ge(s_last_norm[1][k // 2], 4)
                sc.activation(out_last[:, k, :], z2_last[:, k, :], ACT.Identity, scale=norm_last[:, 1, 2, k:k + 1],
                              bias=norm_last[:, 1, 3, k:k + 1]).then_inc(s_last_out, 1)

        @block.vector
        def _(dve):
            v = nc.vector

            def gate_dot(step, tiles=range(TILES)):
                b = step.b
                if not starts(step, 1):
                    dve.wait_ge(s_x[b], (step.j + b) * 16)
                if not starts(step, 2):
                    dve.wait_ge(s_gate, step.after(-2).count())
                for k in tiles:
                    if starts(step, 1) and k % 2 == 0:
                        dve.wait_ge(s_x_first[k // 2], 16)
                    v.tensor_tensor_reduce(out=dot_terms[:, b, k, :], in0=x_tok[b][:, k, :], in1=wg_rows[:, :],
                                           scale=1.0, scalar=0.0, op0=ALU.mult, op1=ALU.add,
                                           accum_out=gate[b][:, 0, k:k + 1]).then_inc(s_dot, 1)

            def scan(step):
                b = step.b
                dve.wait_ge(s_decay, step.count())
                if not starts(step, 2):
                    dve.wait_ge(s_scan, step.after(-2).count(2))
                    dve.wait_ge(s_hidden_hi, step.after(-2).count(2))
                    dve.wait_ge(s_hidden_lo, step.after(-2).count(2))
                for h in range(HALVES):
                    dve.wait_ge(s_gx_t, step.count(2, h + 1))
                    v.tensor_tensor_scan(hidden[b][:, h, :], decay[b][:, :], pair_gx_attn[h][:, :],
                                         hidden[b][:, h, GROUP - 1:GROUP], ALU.mult, ALU.add).then_inc(s_scan, 1)

            def last_residual2(h):
                dve.wait_ge(s_rv, LAST.count(2, h + 1))
                v.tensor_tensor(pair(z2_last, h), pair(rv, h), pair(y_tok[LAST.b], h), ALU.add).then_inc(s_z2, 1)

            def bn_stats(n, z, s_ready, s_st, step, h):
                dve.wait_ge(s_ready, step.count(2, h + 1))
                for k in (2 * h, 2 * h + 1):
                    last = v.bn_stats(stats[:, n, k, :], z[:, k, :])
                last.then_inc(s_st, 1)

            def bn_aggr(n, s_st, s_mom, step):
                dve.wait_ge(s_st, step.count(2))
                v.tensor_copy(settled_dve[:, :], stats[:, n, 0, 0:1])
                for k in range(TILES):
                    last = v.bn_aggr(moments[:, n, k, :], stats[:, n, k, :])
                last.then_inc(s_mom, 1)

            def half_stats(n, z, s_ready, s_st, moments_done, step, part):
                bn_stats(n, z, s_ready, s_st, step, part)
                dve.wait_ge(s_st, step.count(2, part + 1))
                if step is LAST:
                    dve.wait_ge((s_ln1, s_ln2)[n], step.after(-1).count(4, 2))
                for k in (2 * part, 2 * part + 1):
                    last = v.bn_aggr(moments[:, n, k, :], stats[:, n, k, :])
                last.then_inc(moments_done[part], 1)

            def tile_stats(n, z, s_ready, s_st, s_mom, step):
                for h in range(2):
                    bn_stats(n, z, s_ready, s_st, step, h)
                bn_aggr(n, s_st, s_mom, step)

            def residual1(step, h, banks=pair_gx_attn):
                dve.wait_ge(s_attn, step.count(2, h + 1))
                v.tensor_tensor(pair(z1, h), banks[h][:, :], pair(x_tok[step.b], h), ALU.add).then_inc(s_z1, 1)

            def split_k(step, h):
                dve.wait_ge(s_k_hi, step.count(2, h + 1))
                v.tensor_tensor(k_lo[:, h, :], k_act[:, h, :], k_hi[:, h, :].bitcast(F32), ALU.subtract).then_inc(s_k_lo[h], 1)

            def mix(step, n, h):
                dve.wait_ge(s_shift, step.count(2, h + 1))
                v.scalar_tensor_tensor(out=mixed[:, n, h, :], in0=pair_yT_r[h][:, :], scalar=mu[:, n, h:h + 1],
                                       in1=shifted[step.b][:, n, h, 0:GROUP], op0=ALU.mult,
                                       op1=ALU.add).then_inc((s_mix_k, s_mix_r)[n], 1)

            def split_mixed(step, h):
                dve.wait_ge(s_mixed_hi, step.count(2, h + 1))
                v.tensor_tensor(mixed_lo[:, h, :], mixed[:, 0, h, :], mixed_hi[:, h, :].bitcast(F32),
                                ALU.subtract).then_inc(s_mixed_lo[h], 1)

            def half_norm1(step, part, norm_1, small, s_done):
                k = 2 * part + 1
                dve.wait_ge(small[part], 4)
                v.tensor_scalar(y_tok[step.b][:, k, :], z1[:, k, :], norm_1[:, 2, k:k + 1], norm_1[:, 3, k:k + 1],
                                ALU.mult, ALU.add).then_inc(s_done, 1)

            def gate_v(step, h):
                dve.wait_ge(s_v, step.count(2, h + 1))
                dve.wait_ge(s_sig, step.count(2, h + 1))
                v.tensor_tensor(pair(rv, h), pair_k_v[h][:, :], pair(r_gate, h), ALU.mult).then_inc(s_rv, 1)

            def split_hidden(step):
                b = step.b
                for h in range(HALVES):
                    dve.wait_ge(s_hidden_hi, step.count(2, h + 1))
                    v.tensor_tensor(hidden_lo[b][:, h, :], hidden[b][:, h, :], hidden_hi[b][:, h, :].bitcast(F32),
                                    ALU.subtract).then_inc(s_hidden_lo, 1)

            def body(step, to_come):
                before = step.after(-1)
                if starts(step, 1):
                    mix(step, 0, 0)
                    gate_dot(step.after(2), (2, 3))
                    mix(step, 0, 1)
                    mix(step, 1, 0)
                    split_mixed(step, 1)
                    for h in range(2):
                        residual1(step.after(1), h)
                    mix(step, 1, 1)
                else:
                    for h in range(HALVES):
                        for n in range(2):
                            mix(step, n, h)
                    split_mixed(step, 1)
                    if to_come >= 2:
                        for h in range(2):
                            residual1(step.after(1), h)
                if to_come >= 2:
                    tile_stats(0, z1, s_z1, s_st1, s_mom1, step.after(1))
                    scan(step.after(2))
                    split_k(step, 0)
                    if to_come != 3:
                        split_k(step, 1)
                    if not starts(step, 1):
                        tile_stats(1, z2[before.b], s_z2, s_st2, s_mom2, before)
                    gate_v(step, 0)
                    if to_come >= 3:
                        gate_dot(step.after(3), (0, 1))
                    gate_v(step, 1)
                    if to_come >= 3:
                        gate_dot(step.after(3), (2, 3))
                else:
                    for part in range(2):
                        residual1(LAST, part)
                        half_stats(0, z1, s_z1, s_st1, s_last_mom[0], LAST, part)
                    half_norm1(LAST, 0, norm_last[:, 0], s_last_norm[0], s_last_y[1])
                    bn_stats(1, z2[before.b], s_z2, s_st2, before, 0)
                    split_k(step, 0)
                    half_norm1(LAST, 1, norm_last[:, 0], s_last_norm[0], s_last_y[1])
                    split_k(step, 1)
                    bn_stats(1, z2[before.b], s_z2, s_st2, before, 1)
                    bn_aggr(1, s_st2, s_mom2, before)
                    last_mix(0, 0)
                    last_mix(0, 1)
                    last_split_mixed(0)
                    last_mix(1, 0)
                    last_split_mixed(1)
                    gate_v(step, 0)
                    last_mix(1, 1)
                    last_split_k()
                    gate_v(step, 1)

            def last_mix(n, part):
                dve.wait_ge(s_last_shift[n], part + 1)
                tokens = half_tokens(part)
                for h in range(HALVES):
                    last = v.scalar_tensor_tensor(out=mixed[:, n, h, tokens], in0=pair_gx_attn[part][:, half_tokens(h)],
                                                  scalar=mu[:, n, h:h + 1], in1=shifted[LAST.b][:, n, h, tokens],
                                                  op0=ALU.mult, op1=ALU.add)
                last.then_inc((s_mix_k, s_mix_r)[n], 1)

            def last_split_mixed(part):
                dve.wait_ge(s_mixed_hi, LAST.count(2, part + 1))
                tokens = half_tokens(part)
                v.tensor_tensor(mixed_lo[:, :, tokens], mixed[:, 0, :, tokens], mixed_hi[:, :, tokens].bitcast(F32),
                                ALU.subtract).then_inc(s_last_mixed_lo, 1)

            def last_split_k():
                dve.wait_ge(s_k_hi, LAST.count(2, 1))
                tokens = half_tokens(0)
                v.tensor_tensor(k_lo[:, :, tokens], k_act[:, :, tokens], k_hi[:, :, tokens].bitcast(F32),
                                ALU.subtract).then_inc(s_last_k_lo[0], 1)

            def last_step():
                before = LAST.after(-1)
                bn_stats(1, z2[before.b], s_z2, s_st2, before, 0)
                gate_v(LAST, 0)
                bn_stats(1, z2[before.b], s_z2, s_st2, before, 1)
                bn_aggr(1, s_st2, s_mom2, before)
                last_residual2(0)
                half_stats(1, z2_last, s_z2, s_st2, s_last_mom[1], LAST, 0)
                gate_v(LAST, 1)
                last_residual2(1)
                half_stats(1, z2_last, s_z2, s_st2, s_last_mom[1], LAST, 1)
                dve.wait_ge(s_last_norm[1][1], 4)
                k = TILES - 1
                v.tensor_scalar(out_last[:, k, :], z2_last[:, k, :], norm_last[:, 1, 2, k:k + 1], norm_last[:, 1, 3, k:k + 1],
                                ALU.mult, ALU.add).then_inc(s_last_dve, 1)

            v.memset(bout_row[:, :], 0.0).then_inc(s_bias_zero, 1)
            v.memset(ones[:, :].bitcast(F32), 1.0).then_inc(s_ones, 1)
            for b in range(2):
                v.memset(hidden[b][:, :, GROUP - 1:GROUP], 0.0).then_inc(s_zeros, 1)
                v.memset(shifted[b][:, :, :, GROUP:GROUP + 1], 0.0).then_inc(s_zeros, 1)
            dve.wait_ge(s_gate_w, 32)
            for part in range(2):
                gate_dot(Step(0, 0), (2 * part, 2 * part + 1))
            for part in range(2):
                dve.wait_ge(s_first_gate[part], 1)
                for k in (2 * part, 2 * part + 1):
                    last = v.tensor_scalar(gated_x[0][:, k, :], x_tok[0][:, k, :], gate[0][:, 1, k:k + 1], None, ALU.mult)
                last.then_inc(s_first_gx[part], 1)
            dve.wait_ge(s_bias, 1)
            low = slice(LO_ROW, LO_ROW + 1)
            v.tensor_tensor(bout_parts[low, :], bout_row[low, :], bout_parts[low, :].bitcast(F32),
                            ALU.subtract).then_inc(s_bias, 1)
            dve.wait_ge(s_zeros, 4)
            for part in range(2):
                tokens = half_tokens(part)
                dve.wait_ge(s_first_decay[part], 1)
                dve.wait_ge(s_gx_t, part + 1)
                if part == 1:
                    dve.wait_ge(s_scan, 1)
                for h in range(HALVES):
                    last = v.tensor_tensor_scan(hidden[0][:, h, tokens], decay[0][:, tokens],
                                                pair_gx_attn[part][:, half_tokens(h)],
                                                hidden[0][:, h, (tokens.start - 1) % GROUP:(tokens.start - 1) % GROUP + 1],
                                                ALU.mult, ALU.add)
                last.then_inc(s_scan, 1)
            dve.wait_ge(s_hidden_hi, 1)
            v.tensor_tensor(hidden_lo[0][:, :, half_tokens(0)], hidden[0][:, :, half_tokens(0)],
                            hidden_hi[0][:, :, half_tokens(0)].bitcast(F32), ALU.subtract).then_inc(s_first_hidden_lo, 1)
            gate_dot(Step(0, 1))
            dve.wait_ge(s_mu, 16)
            v.tensor_scalar(one_minus_mu[:, :, :], mu[:, :, :], -1.0, 1.0, ALU.mult, ALU.add).then_inc(s_omm, 1)
            for h in range(2):
                residual1(Step(0, 0), h, pair_k_v)
                half_stats(0, z1, s_z1, s_st1, s_first_mom1, Step(0, 0), h)
            half_norm1(Step(0, 0), 0, norm[:, 0], s_first_ln1, s_y)
            scan(Step(0, 1))
            half_norm1(Step(0, 0), 1, norm[:, 0], s_first_ln1, s_y)
            split_hidden(Step(0, 1))
            gate_dot(Step(1, 0), (0, 1))
            all_steps(dve, body)
            last_step()

        @block.tensor
        def _(pe):
            t = nc.tensor

            def transpose_gated(step):
                b = step.b
                pe.wait_ge(s_one_minus, step.count())
                if not starts(step, 2):
                    pe.wait_ge(s_decay, step.after(-2).count())
                if not starts(step, 1) and starts(step, 2):
                    pe.wait_ge(s_decay, 1)
                for k in range(TILES):
                    last = t.transpose(decay_ps[b][:, k * P:(k + 1) * P],
                                       gate[b][:, 2, k:k + 1].to_broadcast([P, P]), ident[:, :])
                last.then_inc(s_decay_t, 1)
                pe.wait_ge(s_gx, step.count())
                if not starts(step, 2):
                    pe.wait_ge(s_z1, step.after(-1).count(2))
                if not starts(step, 1) and starts(step, 2):
                    pe.wait_ge(s_scan, 2)
                for h in range(HALVES):
                    for k in range(TILES):
                        last = t.transpose(pair_gx_attn[h][:, k * P:(k + 1) * P],
                                           gated_x[b][:, k, h * P:(h + 1) * P], ident[:, :])
                    last.then_inc(s_gx_t, 1)

            def first_transpose_gated(part):
                pe.wait_ge(s_first_one_minus[part], 1)
                for k in (2 * part, 2 * part + 1):
                    last = t.transpose(decay_ps[part][:, k * P:(k + 1) * P],
                                       gate[0][:, 2, k:k + 1].to_broadcast([P, P]), ident[:, :])
                last.then_inc(s_first_decay_t[part], 1)
                pe.wait_ge(s_first_gx[part], 1)
                for h in range(HALVES):
                    for k in range(2):
                        last = t.transpose(pair_gx_attn[part][:, (2 * h + k) * P:(2 * h + k + 1) * P],
                                           gated_x[0][:, 2 * part + k, h * P:(h + 1) * P], ident[:, :])
                last.then_inc(s_gx_t, 1)

            def token_product(banks, halves, lhs, w, s_done):
                for h in halves:
                    for k in (2 * h, 2 * h + 1):
                        for c in range(HALVES):
                            last = t.matmul(banks[h][:, (k % 2) * C:(k % 2 + 1) * C], lhs[:, c, k * P:(k + 1) * P],
                                            w[:, c, :], start=(c == 0), stop=(c == HALVES - 1))
                    last.then_inc(s_done, 1)

            def split_token_product(banks, halves, x_hi, x_lo, w_hi, w_lo, lo_done, s_done, bias=False):
                for h in halves:
                    for k in (2 * h, 2 * h + 1):
                        columns = banks[h][:, (k % 2) * C:(k % 2 + 1) * C]
                        if bias:
                            t.matmul(columns, ones[:, :], bout_parts[:, :], start=True, stop=False)
                        for n, (x_part, w_part, c) in enumerate(
                                [(x, w, c) for x, w in ((x_hi, w_lo), (x_hi, w_hi), (x_lo, w_hi)) for c in range(HALVES)]):
                            if k == 2 * h and n == 2 * HALVES:
                                for s_lo, count in lo_done:
                                    pe.wait_ge(s_lo, count)
                            last = t.matmul(columns, x_part[:, c, k * P:(k + 1) * P], w_part[:, c, :],
                                            start=(n == 0 and not bias), stop=(n == 3 * HALVES - 1))
                    last.then_inc(s_done, 1)

            def attn(step):
                pe.wait_ge(s_hidden_hi, step.count(2))
                split_token_product(pair_gx_attn, range(2), hidden_hi[step.b], hidden_lo[step.b], wout_hi, wout_lo,
                                    [(s_hidden_lo, step.count(2))], s_attn, bias=True)

            def first_attn(part):
                pe.wait_ge(s_hidden_hi, part + 1)
                split_token_product(pair_k_v, (part,), hidden_hi[0], hidden_lo[0], wout_hi, wout_lo,
                                    [((s_first_hidden_lo, 1), (s_hidden_lo, 2))[part]], s_attn, bias=True)

            def transpose_y(step):
                pe.wait_ge(s_y, step.count(4))
                for h in range(HALVES):
                    if not starts(step, 1):
                        pe.wait_ge(s_sig, step.after(-1).count(2, h + 1))
                    for k in range(TILES):
                        last = t.transpose(pair_yT_r[h][:, k * P:(k + 1) * P],
                                           y_tok[step.b][:, k, h * P:(h + 1) * P], ident[:, :])
                    last.then_inc(s_yT, 1)

            def k_product(step):
                if starts(step, 1):
                    pe.wait_ge(s_wk_hi, 1)
                    pe.wait_ge(s_wk_lo, 1)
                else:
                    pe.wait_ge(s_rv, step.after(-1).count(2))
                for c in range(HALVES):
                    pe.wait_ge(s_mixed_hi, step.count(2, c + 1))
                    for h in range(HALVES):
                        for w_part in (wk_lo, wk_hi):
                            t.matmul(pair_k_v[h][:, :], w_part[:, c, h * P:(h + 1) * P], mixed_hi[:, c, :],
                                     start=(c == 0 and w_part is wk_lo), stop=False)
                for c in range(HALVES):
                    pe.wait_ge(s_mixed_lo[c], step.count())
                for h in range(HALVES):
                    for c in range(HALVES):
                        last = t.matmul(pair_k_v[h][:, :], wk_hi[:, c, h * P:(h + 1) * P], mixed_lo[:, c, :],
                                        start=False, stop=(c == HALVES - 1))
                    last.then_inc(s_k, 1)

            def r_product(step):
                if starts(step, 1):
                    pe.wait_ge(s_wr, 16)
                pe.wait_ge(s_mix_r, step.count(2))
                token_product(pair_yT_r, range(2), mixed[:, 1], wr, s_r)

            def v_product(step):
                if starts(step, 1):
                    pe.wait_ge(s_wv_hi, 1)
                    pe.wait_ge(s_wv_lo, 1)
                pe.wait_ge(s_k_hi, step.count(2))
                split_token_product(pair_k_v, range(2), k_hi, k_lo, wv_hi, wv_lo,
                                    [(s_done, step.count()) for s_done in s_k_lo], s_v)

            def body(step, to_come):
                transpose_y(step)
                attn(step.after(1))
                k_product(step)
                if to_come >= 2:
                    transpose_gated(step.after(2))
                r_product(step)
                if to_come >= 2:
                    v_product(step)
                else:
                    for part in range(2):
                        last_transpose_y(part)
                    v_product(step)

            def last_transpose_y(part):
                for s_done in s_last_y:
                    pe.wait_ge(s_done, part + 1)
                for h in range(HALVES):
                    for k in range(2):
                        last = t.transpose(pair_gx_attn[part][:, (2 * h + k) * P:(2 * h + k + 1) * P],
                                           y_tok[LAST.b][:, 2 * part + k, h * P:(h + 1) * P], ident[:, :])
                last.then_inc(s_last_yT, 1)

            def last_k_product(part):
                pe.wait_ge(s_sig, LAST.after(-1).count(2, part + 1))
                pe.wait_ge(s_mixed_hi, LAST.count(2, part + 1))
                tokens = half_tokens(part)
                for h in range(HALVES):
                    for n, (w_part, x_part, c) in enumerate(
                            [(w, x, c) for w, x in ((wk_lo, mixed_hi), (wk_hi, mixed_hi), (wk_hi, mixed_lo)) for c in range(HALVES)]):
                        if h == 0 and n == 2 * HALVES:
                            pe.wait_ge(s_last_mixed_lo, part + 1)
                        last = t.matmul(pair_yT_r[part][:, half_tokens(h)], w_part[:, c, h * P:(h + 1) * P], x_part[:, c, tokens],
                                        start=(n == 0), stop=(n == 3 * HALVES - 1))
                last.then_inc(s_k, 1)

            def last_step():
                for part in range(2):
                    last_k_product(part)
                for part in range(2):
                    pe.wait_ge(s_mix_r, LAST.count(2, part + 1))
                    token_product(pair_gx_attn, (part,), mixed[:, 1], wr, s_r)
                    pe.wait_ge(s_rv, LAST.after(-1).count(2, part + 1))
                    pe.wait_ge(s_k_hi, LAST.count(2, part + 1))
                    split_token_product(pair_k_v, (part,), k_hi, k_lo, wv_hi, wv_lo, [(s_last_k_lo[part], 1)], s_v)

            def keep_warm(n):
                for _ in range(n):
                    t.matmul(pair_yT_r[0][:, 0:P], ident[:, :], ident[:, :], start=True, stop=True)

            pe.wait_ge(s_ident, 1)
            keep_warm(WARM_UP[0])
            first_transpose_gated(0)
            first_transpose_gated(1)
            keep_warm(WARM_UP[1])
            pe.wait_ge(s_wout_hi, 1)
            pe.wait_ge(s_wout_lo, 1)
            pe.wait_ge(s_ones, 1)
            pe.wait_ge(s_bias, 2)
            first_attn(0)
            first_attn(1)
            transpose_gated(Step(0, 1))
            keep_warm(WARM_UP[2])
            all_steps(pe, body)
            last_step()


def kernel(L0_attn_x, L0_attn_Wg, L0_attn_bg, L0_attn_Wout, L0_attn_bout, L0_ffn_W_r, L0_ffn_W_k, L0_ffn_W_v,
           L0_ffn_mu_r, L0_ffn_mu_k):
    import numpy as np
    import concourse.bacc as bacc
    from concourse.bass_utils import run_bass_kernel_spmd

    nc = bacc.Bacc("TRN2", target_bir_lowering=False, num_devices=1)
    arrays = {
        "x": L0_attn_x, "Wg": L0_attn_Wg, "bg": L0_attn_bg, "WoutT": np.transpose(L0_attn_Wout), "bout": L0_attn_bout,
        "WrT": np.transpose(L0_ffn_W_r), "WkT": np.transpose(L0_ffn_W_k), "WvT": np.transpose(L0_ffn_W_v),
        "mus": np.transpose(np.stack([L0_ffn_mu_k, L0_ffn_mu_r]).reshape(2, -1, P), (2, 0, 1)),
    }
    arrays = {n: np.ascontiguousarray(a) for n, a in arrays.items()}
    ins = [nc.dram_tensor(n, a.shape, mybir.dt.from_np(a.dtype), kind="ExternalInput").ap() for n, a in arrays.items()]
    out = nc.dram_tensor("out", arrays["x"].shape, F32, kind="ExternalOutput").ap()
    build(nc, *ins, out)
    ran = run_bass_kernel_spmd(nc, [arrays], core_ids=[0])
    return ran.results[0]["out"]
```
